# Optimizing a Trainium2 kernel written in Bass

```python
import numpy as np
import jax
import jax.numpy as jnp

def _softmax(x, axis=-1):
    return jax.nn.softmax(x, axis=axis)

def _gelu(x):
    return jax.nn.gelu(x, approximate=True)

def _silu(x):
    return jax.nn.silu(x)

def _sigmoid(x):
    return jax.nn.sigmoid(x)

def _layernorm(x, axis=-1, eps=1e-05):
    m = jnp.mean(x, axis=axis, keepdims=True)
    v = jnp.var(x, axis=axis, keepdims=True)
    return (x - m) / jnp.sqrt(v + eps)

def _scatter_add(tgt, idx, src, axis=0):
    return tgt.at[idx].add(src)

def _segment_sum(src, seg, n):
    return jax.ops.segment_sum(src, seg, n)
kernel_name = 'mk_adj_preln_d2_adj_r2_f6cdd2'

def setup_inputs(seed: int=0):
    np.random.seed(seed)
    _w = jnp.asarray

    def _rec_inputs():
        import jax
        import jax.numpy as jnp
        _gk = jax.random.key(seed)
        x = -0.000929 + 1 * jax.random.normal(jax.random.fold_in(_gk, 1), (8192, 128), jnp.float32)
        _a = jax.random.bernoulli(jax.random.fold_in(_gk, 2), 0.000976562, (8192, 8192))
        _a = jnp.logical_or(_a, jnp.eye(8192, dtype=bool))
        _af = _a.astype(jnp.float32)
        adj = _af
        return (x, adj)
    x, adj = _rec_inputs()

    def _L0_gnn_setup():
        import jax, jax.numpy as jnp
        import numpy as np
        N = 4096
        D = 128
        EPS = 1e-07
        NEG = -1000000000.0
        key = jax.random.key(seed)
        kx, ka, kb = jax.random.split(key, 3)
        x = jax.random.normal(kx, (N, D), dtype=jnp.float32)
        adj = jax.random.randint(ka, (N, N), 0, 2).astype(jnp.float32)
        adj = adj.at[jnp.arange(N), jnp.arange(N)].set(1.0)
        beta = jax.random.uniform(kb, (1,), dtype=jnp.float32)
        return {'x': x, 'adj': adj, 'beta': beta}
    _L0_gnn_all = _L0_gnn_setup()
    _L0_gnn_in = {k: v for k, v in _L0_gnn_all.items() if k in ('beta',)}
    del _L0_gnn_all

    def _L1_gnn_setup():
        import jax, jax.numpy as jnp
        import numpy as np
        K = 2
        NEG = -9000000000000000.0
        N, C, CO = (3072, 128, 128)

        def _ln(x, g, b, eps=1e-05):
            m = x.mean(-1, keepdims=True)
            v = ((x - m) ** 2).mean(-1, keepdims=True)
            return (x - m) / jnp.sqrt(v + eps) * g + b
        key = jax.random.key(seed)
        ks = jax.random.split(key, 6)
        x = jax.random.normal(ks[0], (N, C), jnp.float32)
        adj = (jax.random.uniform(ks[1], (N, N)) < 0.01).astype(jnp.float32)
        ff0_w = jax.random.normal(ks[2], (K, C, C), jnp.float32) / np.float32(np.sqrt(C))
        ff1_w = jax.random.normal(ks[3], (K, CO, C), jnp.float32) / np.float32(np.sqrt(C))
        attn_w = jax.random.normal(ks[4], (K, 2 * C), jnp.float32) / np.float32(np.sqrt(2 * C))
        return dict(x=x, adj=adj, ff0_w=ff0_w, ff1_w=ff1_w, attn_w=attn_w, g1=jnp.ones((C,), jnp.float32), b1=jnp.zeros((C,), jnp.float32), g2=jnp.ones((C,), jnp.float32), b2=jnp.zeros((C,), jnp.float32))
    _L1_gnn_all = _L1_gnn_setup()
    _L1_gnn_in = {k: v for k, v in _L1_gnn_all.items() if k in ('ff0_w', 'ff1_w', 'attn_w', 'g1', 'b1', 'g2', 'b2')}
    del _L1_gnn_all
    return {'x': x, 'adj': adj, 'L0_gnn_beta': _L0_gnn_in['beta'], 'L1_gnn_ff0_w': _L1_gnn_in['ff0_w'], 'L1_gnn_ff1_w': _L1_gnn_in['ff1_w'], 'L1_gnn_attn_w': _L1_gnn_in['attn_w'], 'L1_gnn_g1': _L1_gnn_in['g1'], 'L1_gnn_b1': _L1_gnn_in['b1'], 'L1_gnn_g2': _L1_gnn_in['g2'], 'L1_gnn_b2': _L1_gnn_in['b2']}

def reference(x, adj, L0_gnn_beta, L1_gnn_ff0_w, L1_gnn_ff1_w, L1_gnn_attn_w, L1_gnn_g1, L1_gnn_b1, L1_gnn_g2, L1_gnn_b2):
    import jax
    import jax.numpy as jnp

    def _L0_gnn_ref(x, adj, beta):
        import jax, jax.numpy as jnp
        import numpy as np
        N = 4096
        D = 128
        EPS = 1e-07
        NEG = -1000000000.0
        norm2 = jnp.linalg.norm(x, axis=1, keepdims=True)
        cos = beta * (x @ x.T) / (norm2 @ norm2.T + EPS)
        masked = cos + (1.0 - adj) * NEG
        P = jax.nn.softmax(masked, axis=1)
        return P @ x

    def _L1_gnn_ref(x, adj, ff0_w, ff1_w, attn_w, g1, b1, g2, b2):
        import jax, jax.numpy as jnp
        import numpy as np
        K = 2
        NEG = -9000000000000000.0
        N, C, CO = (3072, 128, 128)

        def _ln(x, g, b, eps=1e-05):
            m = x.mean(-1, keepdims=True)
            v = ((x - m) ** 2).mean(-1, keepdims=True)
            return (x - m) / jnp.sqrt(v + eps) * g + b
        n, c = x.shape
        co = ff1_w.shape[1]
        x_norm = _ln(x, g1, b1)
        mask = (adj > 0) | jnp.eye(n, dtype=bool)
        h_next = jnp.zeros((n, co), x.dtype)
        for i in range(K):
            h = x_norm @ ff0_w[i].T
            s_src = h @ attn_w[i, :c]
            s_dst = h @ attn_w[i, c:]
            e = jax.nn.leaky_relu(s_src[:, None] + s_dst[None, :])
            e = jnp.where(mask, e, jnp.float32(NEG))
            atten = jax.nn.softmax(e, axis=1)
            att = atten @ h + x
            att = _ln(att, g2, b2)
            h_next = h_next + jax.nn.elu(att @ ff1_w[i].T) / K
        return h_next
    h = jnp.maximum(_layernorm(x, axis=-1), 0.0)
    x = x + _L0_gnn_ref(h, adj, L0_gnn_beta)
    h = jnp.maximum(_layernorm(x, axis=-1), 0.0)
    x = x + _L1_gnn_ref(h, adj, L1_gnn_ff0_w, L1_gnn_ff1_w, L1_gnn_attn_w, L1_gnn_g1, L1_gnn_b1, L1_gnn_g2, L1_gnn_b2)
    return x

_drawn_inputs = setup_inputs


def setup_inputs(seed=0):
    import zlib

    import numpy as np

    out = dict(_drawn_inputs(seed))
    spreads = {'L1_gnn_g1': (1.0, 0.2),
     'L1_gnn_b1': (0.0, 0.1),
     'L1_gnn_g2': (1.0, 0.2),
     'L1_gnn_b2': (0.0, 0.1)}
    factors = {}
    for name, (base, spread) in spreads.items():
        noise = np.random.default_rng([zlib.crc32(name.encode()), seed]).standard_normal(out[name].shape)
        drawn = base * np.exp(spread * noise) if base else spread * noise
        out[name] = jnp.asarray(drawn.astype(out[name].dtype))
    for name, factor in factors.items():
        out[name] = (out[name] * factor).astype(out[name].dtype)
    return out
```

```python
from contextlib import ExitStack

import concourse.bass as bass
from concourse import mybir

ALU = mybir.AluOpType
ACT = mybir.ActivationFunctionType
AX_X = mybir.AxisListType.X
F32 = mybir.dt.float32
F16 = mybir.dt.float16
ds = bass.ds

P = 128
TPB = 4
BLK = TPB * P
GJ = 4
SLOTS = 2
UNR = GJ * SLOTS
LAG = 2
PRING = 4
NORM_EPS = 1e-7
LN_EPS = 1e-5
SLOPE = 0.01
XSC = 64.0
SEGS = [(1, 3), (3, 5), (5, 6), (6, 8)]


def adj_prenorm_two_layers(nc, x, adj, beta, ff0_w, ff1_w, attn_w, g1, b1, g2, b2, out):
    N, D = x.shape
    K = ff0_w.shape[0]
    NT = N // P
    NB = N // BLK
    NQ = NT // UNR
    NCH = NQ
    VW = D + 1
    HW = K * VW + K
    S1 = NB * NT
    KT = K * TPB
    EP0, EP1 = 8, 6
    assert D == P and K == 2 and N % BLK == 0 and SEGS[-1][1] == NQ

    x_t = x.rearrange("(t p) d -> p t d", p=P)
    adj_t = adj.rearrange("(t p) c -> p t c", p=P)
    out_t = out.rearrange("(t p) d -> p t d", p=P)
    x1_d = nc.dram_tensor("x1_scratch", [N, D], F32, kind="Internal").ap()
    h1_d = nc.dram_tensor("h1_scratch", [N, D], F32, kind="Internal").ap()
    a_d = nc.dram_tensor("src_scratch", [K, N], F32, kind="Internal").ap()
    x1_t = x1_d.rearrange("(t p) d -> p t d", p=P)
    h1_t = h1_d.rearrange("(t p) d -> p t d", p=P)

    with ExitStack() as ctx:
        def sb(name, shape, dt=F32):
            return ctx.enter_context(nc.sbuf_tensor(name, shape, dt))

        def pb(name, shape):
            return ctx.enter_context(nc.psum_tensor(name, shape, F32))

        def sem(name):
            return ctx.enter_context(nc.semaphore(name))

        ident = sb("ident", [P, P])
        ones = sb("ones", [P, P])
        neg_half = sb("neg_half", [P, UNR])
        eps_t = sb("eps_t", [P, UNR])
        w0n = sb("w0n", [P, K, D])
        w1n = sb("w1n", [P, K, D])
        attn_c = sb("attn_c", [P, K, 2])
        ln_par = sb("ln_par", [P, 4])
        w_h = sb("w_h", [P, HW])
        w1T = sb("w1T", [P, K, D])
        beta_c = sb("beta_c", [P, 1])
        beta_s = sb("beta_s", [P, 1])
        beta_n = sb("beta_n", [P, 1])
        beta_m = sb("beta_m", [P, 1])

        carrier = sb("carrier", [P, 64])

        xT_hi = sb("xT_hi", [P, N], F16)
        xT_lo = sb("xT_lo", [P, N], F16)
        v0 = sb("v0", [P, NT, VW])
        v1 = sb("v1", [P, NT, HW])
        vsum = sb("vsum", [P, VW])

        adj_sb = sb("adj_sb", [P, SLOTS, TPB, GJ * P])
        e_sb = sb("e_sb", [P, 2, BLK])
        p_sb = sb("p_sb", [P, PRING, K, BLK])

        v1_flat = v1[:, :, :].rearrange("p t d -> p (t d)")

        def room(flat, start, *dims):
            n = 1
            for d in dims:
                n *= d
            v = flat[:, start:start + n]
            names = "abcd"[:len(dims)]
            return v.rearrange(f"p ({' '.join(names)}) -> p {' '.join(names)}", **dict(zip(names, dims)))

        CW = UNR * D
        xin = room(v1_flat, 0, 2, UNR, D)
        y_c = room(v1_flat, 2 * CW, UNR, D)
        sq_c = room(v1_flat, 3 * CW, UNR, D)
        xhat = room(v1_flat, 4 * CW, 2, UNR, D)
        st6 = sb("st6", [P, UNR, 6])
        st2 = sb("st2", [P, UNR, 2])
        veps = sb("veps", [P, UNR])
        rstd = sb("rstd", [P, UNR])
        n2 = sb("n2", [P, UNR])
        n2e = sb("n2e", [P, UNR])
        rn = sb("rn", [P, UNR])

        oc = sb("oc", [P, KT, VW])
        zrow = sb("zrow", [P, TPB])
        rl = sb("rl", [P, KT])
        xb = sb("xb", [P, TPB, D])
        hb = sb("hb", [P, TPB, D])
        ta = sb("ta", [P, KT, D])
        tb = sb("tb", [P, KT, D])
        es6 = sb("es6", [P, KT, 6])
        es2 = sb("es2", [P, KT, 2])
        ever = sb("ever", [P, KT])
        erstd = sb("erstd", [P, KT])
        lnT = sb("lnT", [P, K, BLK])
        arow = sb("arow", [K, BLK])

        adj_diag = sb("adj_diag", [P, NT])
        bm = sb("bm", [P, K])
        bmx = sb("bmx", [K, 1])
        bdiag = sb("bdiag", [K, K])
        bmax = sb("bmax", [P, 3, K])
        vall = sb("vall", [P, K, NT])
        call = sb("call", [P, K, NT])
        wnat = sb("wnat", [P, K, NT])
        delta = sb("delta", [P, NT])
        coef = sb("coef", [P, K, NT])

        v0_flat = v0[:, :, :].rearrange("p t d -> p (t d)")
        KB = K * BLK
        w_bc = room(v0_flat, 0, 2 * K, BLK)
        a_bc = room(v0_flat, 2 * KB, K, BLK)
        ymin = room(v0_flat, 3 * KB, TPB, K, D)
        yexp = room(v0_flat, 4 * KB, TPB, K, D)
        elu = room(v0_flat, 5 * KB, TPB, K, D)
        ob = room(v0_flat, 6 * KB, TPB, D)

        maskT = pb("maskT", [P, 2, BLK])
        acc = pb("acc", [P, 4, BLK])
        aux = pb("aux", [P, 2, BLK])

        scores = acc[:, 0:2, :]

        def acc0(t):
            return acc[:, 2 + t // 2, (t % 2) * VW:(t % 2 + 1) * VW]

        def acc1(k, t):
            return acc[:, 2 * k + t // 2, (t % 2) * VW:(t % 2 + 1) * VW]

        ident_set, const_set = sem("ident_set"), sem("const_set")
        params_in, diag_in = sem("params_in"), sem("diag_in")
        wprep_mm, wprep_cp = sem("wprep_mm"), sem("wprep_cp")
        beta_neg, beta_ready = sem("beta_neg"), sem("beta_ready")
        adj_in = [sem(f"adj_in{i}") for i in range(SLOTS)]
        x_in = [sem(f"x_in{i}") for i in range(2)]
        st6_done, st2_done = sem("st6_done"), sem("st2_done")
        veps_done, rstd_done = sem("veps_done"), sem("rstd_done")
        y_done, h_done, sq_done = sem("y_done"), sem("h_done"), sem("sq_done")
        n2_done, n2e_done, rn_done = sem("n2_done"), sem("n2e_done"), sem("rn_done")
        xhat_done, xT_psum = sem("xhat_done"), sem("xT_psum")
        hi_done, lo_done = sem("hi_done"), sem("lo_done")
        vsum_mm, vsum_done = sem("vsum_mm"), sem("vsum_done")
        mask_done = sem("mask_done")
        scores_done = sem("scores_done")
        exp_done = sem("exp_done")
        p_made = sem("p_made")
        pv_done = sem("pv_done")
        z_done, oc_done, rl_done = sem("z_done"), sem("oc_done"), sem("rl_done")
        x_blk_in, x1_done, h1_done = sem("x_blk_in"), sem("x1_done"), sem("h1_done")
        ep_chain = sem("ep_chain")
        es6_done, es2_done = sem("es6_done"), sem("es2_done")
        ln_done, lnT_psum, lnT_done = sem("ln_done"), sem("lnT_psum"), sem("lnT_done")
        arow_mm, arow_done = sem("arow_mm"), sem("arow_done")
        h_mm, h_cp = sem("h_mm"), sem("h_cp")
        x1_out, h1_out, a_out = sem("x1_out"), sem("h1_out"), sem("a_out")
        bm_done, bm_T, bmx_done, bdiag_done, bmax_mm, bmax_done = (
            sem("bm_done"), sem("bm_T"), sem("bmx_done"), sem("bdiag_done"), sem("bmax_mm"), sem("bmax_done"))
        factors_done, own_done = sem("factors_done"), sem("own_done")
        v1_scaled = [sem("v1_scaled_h0"), sem("v1_scaled_h1")]
        a_in, w_done = sem("a_in"), sem("w_done")
        oc1_done, rl1_done = sem("oc1_done"), sem("rl1_done")
        x1_back, h1_back = sem("x1_back"), sem("h1_back")
        ep1_chain = sem("ep1_chain")
        att_done = sem("att_done")
        fs6_done, fs2_done = sem("fs6_done"), sem("fs2_done")
        ln1_done, attT_psum, attT_done = sem("ln1_done"), sem("attT_psum"), sem("attT_done")
        y_mm, ymin_done, yexp_done, elu_done = sem("y_mm"), sem("ymin_done"), sem("yexp_done"), sem("elu_done")
        ob_done, out_stored = sem("ob_done"), sem("out_stored")

        block = ctx.enter_context(nc.Block())

        carriers = iter(range(64))

        def wait_here(eng, s, value):
            c = next(carriers)
            eng.wait_ge(s, value)
            if eng is nc.vector:
                eng.tensor_copy(carrier[:, c:c + 1], ones[:, 0:1])
            else:
                eng.tensor_tensor(carrier[:, c:c + 1], ones[:, 0:1], ones[:, 0:1], ALU.add)

        def bc(v, n, w=D):
            return v.rearrange("p (t a) -> p t a", a=1).to_broadcast([P, n, w])

        @block.sync
        def _(sp):
            def load_x(c):
                if c >= 2:
                    sp.wait_ge(y_done, c - 1)
                sp.dma_start(xin[:, c % 2], x_t[:, c * UNR:(c + 1) * UNR, :]).then_inc(x_in[c % 2], 16)

            def load_adj(blk, g, slot):
                sp.dma_start(adj_sb[:, slot], adj_t[:, ds(blk * TPB, TPB), ds(g * (GJ * P), GJ * P)])\
                    .then_inc(adj_in[slot], 16)

            load_x(0)
            load_x(1)
            with nc.allow_non_contiguous_dma(reason="small vectors onto partitions"):
                sp.dma_start(beta_c[:], beta.rearrange("(a b) -> a b", a=1).to_broadcast([P, 1]))\
                    .then_inc(params_in, 16)
                sp.dma_start(w0n[:], ff0_w.rearrange("k o c -> o k c")).then_inc(params_in, 16)
                sp.dma_start(w1n[:], ff1_w.rearrange("k o c -> o k c")).then_inc(params_in, 16)
                sp.dma_start(attn_c[:], attn_w.rearrange("k (h o) -> o k h", h=2)).then_inc(params_in, 16)
                for i, v in enumerate((g1, b1, g2, b2)):
                    sp.dma_start(ln_par[:, i:i + 1], v.rearrange("(c a) -> c a", a=1)).then_inc(params_in, 16)
            for slot in range(SLOTS):
                load_adj(0, slot, slot)
            for c in range(2, NCH):
                load_x(c)

            def refill(bp, q, blk, g0):
                for slot in range(SLOTS):
                    sp.wait_ge(mask_done, bp * NT + (q - 1) * UNR + (slot + 1) * GJ)
                    load_adj(blk, g0 + slot, slot)

            with sp.Fori(0, 2 * NB - 1) as bp:
                with sp.Fori(1, NQ) as q:
                    refill(bp, q, bp % NB, q * SLOTS)
                refill(bp, NQ, (bp + 1) % NB, 0)
            with sp.Fori(1, NQ) as q:
                refill(2 * NB - 1, q, NB - 1, q * SLOTS)

        @block.gpsimd
        def _(pool):
            pool.memset(ident[:], 0.0).then_inc(ident_set, 1)
            pool.memset(ones[:], 1.0).then_inc(const_set, 1)
            pool.memset(neg_half[:], -0.5).then_inc(const_set, 1)
            pool.memset(eps_t[:], LN_EPS).then_inc(const_set, 1)
            pool.memset(v0[:, :, D:VW], 1.0).then_inc(const_set, 1)
            pool.wait_ge(ident_set, 1)
            pool.affine_select(out=ident[:], in_=ident[:], compare_op=ALU.not_equal, fill=1.0, base=0,
                               pattern=[[-1, P]], channel_multiplier=1).then_inc(ident_set, 1)
            with nc.allow_non_contiguous_dma(reason="the diagonal of adj"):
                pool.dma_start(adj_diag[:], bass.AP(tensor=adj.tensor, offset=0,
                               ap=[[N + 1, P], [(N + 1) * P, NT]])).then_inc(diag_in, 16)
            pool.wait_ge(const_set, 4)

            def load_a(blk):
                pool.dma_start(a_bc[:, :, :], a_d[:, ds(blk * BLK, BLK)].rearrange("(o k) n -> o k n", o=1)
                               .to_broadcast([P, K, BLK])).then_inc(a_in, 16)

            def link(ins, s, value, carry=False):
                ins.then_inc(s, 1)
                if carry:
                    wait_here(pool, s, value)
                else:
                    pool.wait_ge(s, value)

            for c in range(NCH):
                pool.wait_ge(st2_done, (c + 1) * UNR)
                if c:
                    pool.wait_ge(y_done, c)
                link(pool.tensor_scalar(veps[:], st2[:, :, 1], LN_EPS, None, ALU.add), veps_done, c + 1)
                pool.tensor_tensor(rstd[:], veps[:], neg_half[:], ALU.pow).then_inc(rstd_done, 1)
                pool.wait_ge(n2_done, c + 1)
                link(pool.tensor_scalar(n2e[:], n2[:], NORM_EPS, None, ALU.add), n2e_done, c + 1)
                link(pool.tensor_tensor(rn[:], n2e[:], neg_half[:], ALU.pow), rn_done, c + 1)
                if c >= 2:
                    pool.wait_ge(xT_psum, 2 * (c - 1))
                pool.tensor_tensor(xhat[:, c % 2], v0[:, c * UNR:(c + 1) * UNR, 0:D], bc(rn[:], UNR),
                                   ALU.mult).then_inc(xhat_done, 1)

            def epilogue0(n, blk):
                steps = [0]

                def chain(ins, carry=False):
                    steps[0] += 1
                    link(ins, ep_chain, (n - 1) * EP0 + steps[0], carry)

                def inverse_deviations():
                    chain(pool.tensor_tensor(ever[:, 0:TPB], es2[:, 0:TPB, 1], eps_t[:, 0:TPB], ALU.add))
                    chain(pool.tensor_tensor(erstd[:, 0:TPB], ever[:, 0:TPB], neg_half[:, 0:TPB], ALU.pow))

                pool.dma_start(xb[:], x_t[:, ds(blk * TPB, TPB), :]).then_inc(x_blk_in, 16)
                pool.wait_ge(rl_done, n)
                chain(pool.tensor_tensor(ta[:, 0:TPB], oc[:, 0:TPB, 0:D], bc(rl[:, 0:TPB], TPB), ALU.mult))
                pool.wait_ge(x_blk_in, n * 16)
                link(pool.tensor_tensor(xb[:], ta[:, 0:TPB], xb[:], ALU.add), x1_done, n, True)
                pool.dma_start(x1_t[:, ds(blk * TPB, TPB), :], xb[:]).then_inc(x1_out, 16)
                pool.wait_ge(es2_done, n * (2 * TPB) - TPB)
                inverse_deviations()
                chain(pool.tensor_tensor(ta[:, 0:TPB], xb[:], bc(es2[:, 0:TPB, 0], TPB), ALU.subtract))
                chain(pool.tensor_tensor(tb[:, 0:TPB], ta[:, 0:TPB], bc(erstd[:, 0:TPB], TPB), ALU.mult), True)
                link(pool.tensor_scalar(hb[:], tb[:, 0:TPB], 0.0, None, ALU.max), h1_done, n, True)
                pool.dma_start(h1_t[:, ds(blk * TPB, TPB), :], hb[:]).then_inc(h1_out, 16)
                pool.wait_ge(es2_done, n * (2 * TPB))
                inverse_deviations()
                chain(pool.tensor_tensor(ta[:, 0:TPB], hb[:], bc(es2[:, 0:TPB, 0], TPB), ALU.subtract))
                pool.tensor_tensor(tb[:, 0:TPB], ta[:, 0:TPB], bc(erstd[:, 0:TPB], TPB), ALU.mult)\
                    .then_inc(ln_done, 1)
                wait_here(pool, arow_done, n)
                pool.dma_start(a_d[:, ds(blk * BLK, BLK)], arow[:]).then_inc(a_out, 16)
                pool.wait_ge(x1_out, n * 16)
                pool.wait_ge(h1_out, n * 16)
                wait_here(pool, a_out, n * 16)
                assert steps[0] == EP0

            with pool.Fori(0, NB) as blk:
                epilogue0(blk + 1, blk)

            pool.wait_ge(pv_done, S1 + PRING)
            load_a(0)
            pool.wait_ge(factors_done, 3 * K)
            for c in range(NCH):
                hv = v1[:, c * UNR:(c + 1) * UNR, VW:VW + D]
                pool.tensor_tensor(hv, hv, bc(vall[:, 1, c * UNR:(c + 1) * UNR], UNR), ALU.mult)\
                    .then_inc(v1_scaled[1], 1)

            def epilogue1(n, blk, more):
                steps = [0]

                def chain(ins, carry=False):
                    steps[0] += 1
                    link(ins, ep1_chain, (n - 1) * EP1 + steps[0], carry)

                pool.dma_start(xb[:], x1_t[:, ds(blk * TPB, TPB), :]).then_inc(x1_back, 16)
                pool.dma_start(hb[:], h1_t[:, ds(blk * TPB, TPB), :]).then_inc(h1_back, 16)
                if more:
                    wait_here(pool, w_done, (n + 1) * K)
                    load_a(n + 1)
                pool.wait_ge(rl1_done, n)
                chain(pool.tensor_tensor(ta[:], oc[:, :, 0:D], bc(rl[:], KT), ALU.mult))
                pool.wait_ge(h1_back, n * 16)
                for k in range(K):
                    pool.tensor_tensor(ta[:, k * TPB:(k + 1) * TPB], ta[:, k * TPB:(k + 1) * TPB], hb[:],
                                       ALU.add).then_inc(att_done, 1)
                pool.wait_ge(fs2_done, n * KT)
                chain(pool.tensor_tensor(ever[:], es2[:, :, 1], eps_t[:, 0:KT], ALU.add))
                chain(pool.tensor_tensor(erstd[:], ever[:], neg_half[:, 0:KT], ALU.pow))
                chain(pool.tensor_tensor(ta[:], ta[:], bc(es2[:, :, 0], KT), ALU.subtract))
                pool.tensor_tensor(tb[:], ta[:], bc(erstd[:], KT), ALU.mult).then_inc(ln1_done, 1)
                pool.wait_ge(elu_done, n)
                chain(pool.tensor_tensor(ob[:], elu[:, :, 0, :], elu[:, :, 1, :], ALU.add), True)
                chain(pool.tensor_scalar(ob[:], ob[:], 1.0 / K, -1.0, ALU.mult, ALU.add))
                pool.wait_ge(x1_back, n * 16)
                link(pool.tensor_tensor(ob[:], ob[:], xb[:], ALU.add), ob_done, n, True)
                pool.dma_start(out_t[:, ds(blk * TPB, TPB), :], ob[:]).then_inc(out_stored, 16)
                wait_here(pool, out_stored, n * 16)
                assert steps[0] == EP1

            pool.wait_ge(w_done, K)
            load_a(1)
            with pool.Fori(0, NB - 2) as blk:
                epilogue1(blk + 1, blk, True)
            epilogue1(NB - 1, NB - 2, False)
            epilogue1(NB, NB - 1, False)

        @block.scalar
        def _(act):
            act.wait_ge(wprep_mm, 1)
            for k in range(K):
                act.copy(w_h[:, k * VW:k * VW + D], aux[:, 0, k * P:(k + 1) * P]).then_inc(wprep_cp, 1)
                src, dst = K * P + 2 * k, K * P + 2 * k + 1
                act.copy(w_h[:, k * VW + D:(k + 1) * VW], aux[:, 0, dst:dst + 1]).then_inc(wprep_cp, 1)
                act.copy(w_h[:, K * VW + k:K * VW + k + 1], aux[:, 0, src:src + 1]).then_inc(wprep_cp, 1)
            act.wait_ge(wprep_mm, 2)
            act.copy(w1T[:].rearrange("p k d -> p (k d)"), aux[:, 1, 0:K * D]).then_inc(wprep_cp, 1)

            for c in range(NCH):
                act.wait_ge(h_done, c + 1)
                if c:
                    act.wait_ge(n2_done, c)
                act.activation(sq_c, v0[:, c * UNR:(c + 1) * UNR, 0:D], ACT.Square).then_inc(sq_done, 1)
                for j in range(2):
                    act.wait_ge(xT_psum, 2 * c + j + 1)
                    col = (2 * c + j) * BLK
                    act.activation(xT_hi[:, col:col + BLK], acc[:, j, :], ACT.Copy, scale=XSC).then_inc(hi_done, 1)
            act.wait_ge(beta_ready, 2)

            def turn0(b, q):
                for u in range(UNR):
                    s = b * NT + q * UNR + u
                    act.wait_ge(scores_done, s + 1)
                    act.wait_ge(p_made, s + 1)
                    act.activation(e_sb[:, u % 2, :], scores[:, u % 2, :], ACT.Exp, bias=beta_n[:, 0:1],
                                   scale=beta_s[:, 0:1]).then_inc(exp_done, 1)

            def normalised(n, k, psum, gain):
                return act.activation(lnT[:, k, :], psum, ACT.Identity, bias=ln_par[:, gain + 1:gain + 2],
                                      scale=ln_par[:, gain:gain + 1])

            def ep0_norm(n):
                act.wait_ge(lnT_psum, n)
                normalised(n, 0, aux[:, 0, :], 0).then_inc(lnT_done, 1)

            def ep0_arow(n):
                act.wait_ge(arow_mm, n)
                act.copy(arow[:], aux[0:K, 1, :]).then_inc(arow_done, 1)

            def ep0_rows(n, t):
                act.wait_ge(h_mm, (n - 1) * TPB + t + 1)
                act.copy(v1_flat[:, ds(((n - 1) * TPB + t) * HW, HW)], aux[:, t % 2, 0:HW]).then_inc(h_cp, 1)

            def block0(b, first):
                turn0(b, 0)
                for i, (lo, hi) in enumerate(SEGS):
                    with act.Fori(lo, hi) as q:
                        turn0(b, q)
                    if first:
                        continue
                    if i == 1:
                        ep0_norm(b)
                    elif i == 2:
                        ep0_arow(b)
                        ep0_rows(b, 0)
                    elif i == 3:
                        for t in range(1, TPB):
                            ep0_rows(b, t)

            block0(0, True)
            with act.Fori(1, NB) as b:
                block0(b, False)
            ep0_norm(NB)
            ep0_arow(NB)
            for t in range(TPB):
                ep0_rows(NB, t)

            act.wait_ge(bmax_done, 3)
            for k in range(K):
                act.activation(vall[:, k, :], v1[:, :, k * VW + D], ACT.Exp, bias=bmax[:, 1, k:k + 1], scale=1.0)\
                    .then_inc(factors_done, 1)
                act.activation(call[:, k, :], v1[:, :, k * VW + D], ACT.Exp, bias=bmax[:, 2, k:k + 1],
                               scale=-(1.0 - SLOPE)).then_inc(factors_done, 1)
                act.activation(wnat[:, k, :], v1[:, :, K * VW + k], ACT.Exp, bias=bmax[:, 2, k:k + 1],
                               scale=1.0 - SLOPE).then_inc(factors_done, 1)

            def w_block(b):
                act.wait_ge(a_in, (b + 1) * 16)
                for k in range(K):
                    act.activation(v0_flat[:, ds((b % 2) * KB + k * BLK, BLK)], a_bc[:, k, :], ACT.Exp,
                                   bias=bmax[:, 2, k:k + 1], scale=1.0 - SLOPE).then_inc(w_done, 1)

            def ep1(n):
                act.wait_ge(attT_psum, n)
                for k in range(K):
                    normalised(n, k, aux[:, k, :], 2).then_inc(attT_done, 1)
                act.wait_ge(ymin_done, n)
                act.activation(yexp, ymin, ACT.Exp).then_inc(yexp_done, 1)

            w_block(0)
            w_block(1)
            with act.Fori(1, NB - 1) as n:
                act.wait_ge(p_made, S1 + n * NT + 2)
                w_block(n + 1)
                ep1(n)
            ep1(NB - 1)
            ep1(NB)

        @block.vector
        def _(dve):
            dve.sem_inc(p_made, 2)
            dve.wait_ge(const_set, 4)
            dve.wait_ge(params_in, 8 * 16)
            dve.tensor_scalar(beta_m[:], beta_c[:], -1.0, None, ALU.mult).then_inc(beta_neg, 1)
            dve.tensor_scalar(beta_s[:], beta_c[:], 1.0 / (XSC * XSC), None, ALU.mult).then_inc(beta_ready, 1)
            dve.wait_ge(beta_neg, 1)
            dve.tensor_tensor(beta_n[:], beta_m[:], beta_c[:], ALU.min).then_inc(beta_ready, 1)

            def stats(src, n_tiles, six, two, s6, s2, value6):
                for t in range(n_tiles):
                    dve.bn_stats(six[:, t, :], src[:, t, :]).then_inc(s6, 1)
                wait_here(dve, s6, value6)
                for t in range(n_tiles):
                    dve.bn_aggr(two[:, t, :], six[:, t, :]).then_inc(s2, 1)

            def low_halves(c):
                for j in range(2):
                    dve.wait_ge(hi_done, 2 * c + j + 1)
                    col = (2 * c + j) * BLK
                    dve.scalar_tensor_tensor(out=xT_lo[:, col:col + BLK], in0=acc[:, j, :], scalar=XSC,
                                             in1=xT_hi[:, col:col + BLK], op0=ALU.mult, op1=ALU.subtract)\
                        .then_inc(lo_done, 1)

            for c in range(NCH):
                dve.wait_ge(x_in[c % 2], (c // 2 + 1) * 16)
                stats(xin[:, c % 2], UNR, st6, st2, st6_done, st2_done, (c + 1) * UNR)
                dve.wait_ge(rstd_done, c + 1)
                for t in range(UNR):
                    ins = dve.tensor_scalar(y_c[:, t, :], xin[:, c % 2, t, :], st2[:, t, 0:1], rstd[:, t:t + 1],
                                            ALU.subtract, ALU.mult)
                ins.then_inc(y_done, 1)
                dve.wait_ge(y_done, c + 1)
                dve.tensor_scalar(v0[:, c * UNR:(c + 1) * UNR, 0:D], y_c, 0.0, None, ALU.max).then_inc(h_done, 1)
                dve.wait_ge(sq_done, c + 1)
                dve.tensor_reduce(n2[:], sq_c, AX_X, ALU.add).then_inc(n2_done, 1)
                if c:
                    low_halves(c - 1)
            low_halves(NCH - 1)
            dve.wait_ge(vsum_mm, 1)
            dve.tensor_copy(vsum[:], acc[:, 2, 0:VW]).then_inc(vsum_done, 1)

            def turn0(b, q, after=None):
                for u in range(UNR):
                    s = b * NT + q * UNR + u
                    dve.wait_ge(exp_done, s + 1)
                    dve.wait_ge(mask_done, s + 1)
                    dve.wait_ge(pv_done, s + 1)
                    dve.tensor_tensor(p_sb[:, u % PRING, 0, :], e_sb[:, u % 2, :], maskT[:, u % 2, :], ALU.mult)\
                        .then_inc(p_made, 1)
                    if u == LAG - 1 and after:
                        after()

            def evacuate0(n):
                dve.wait_ge(pv_done, n * NT + PRING)
                weights = acc[:, 2:4, 0:2 * VW].rearrange("p b (t d) -> p b t d", t=2)[:, :, :, D]
                dve.tensor_scalar(zrow[:].rearrange("p (b t) -> p b t", t=2), weights, 0.0, None, ALU.is_equal)\
                    .then_inc(z_done, 1)
                dve.wait_ge(z_done, n)
                for t in range(TPB):
                    dve.scalar_tensor_tensor(out=oc[:, t, :], in0=vsum[:], scalar=zrow[:, t:t + 1], in1=acc0(t),
                                             op0=ALU.mult, op1=ALU.add).then_inc(oc_done, 1)
                dve.wait_ge(oc_done, n * TPB)
                dve.reciprocal(rl[:, 0:TPB], oc[:, 0:TPB, D]).then_inc(rl_done, 1)

            def stats_x1(n):
                dve.wait_ge(x1_done, n)
                stats(xb, TPB, es6, es2, es6_done, es2_done, n * (2 * TPB) - TPB)

            def stats_h1(n):
                dve.wait_ge(h1_done, n)
                stats(hb, TPB, es6, es2, es6_done, es2_done, n * (2 * TPB))

            turn0(0, 0)
            with dve.Fori(1, NQ) as q:
                turn0(0, q)
            with dve.Fori(1, NB) as b:
                turn0(b, 0, lambda: evacuate0(b))
                stats_x1(b)
                for i, (lo, hi) in enumerate(SEGS):
                    with dve.Fori(lo, hi) as q:
                        turn0(b, q)
                    if i == 0:
                        stats_h1(b)
            evacuate0(NB)
            stats_x1(NB)
            stats_h1(NB)

            dve.wait_ge(h_cp, NB * TPB)
            for k in range(K):
                dve.tensor_reduce(bm[:, k:k + 1], v1[:, :, k * VW + D], AX_X, ALU.max).then_inc(bm_done, 1)
            dve.wait_ge(bm_T, 1)
            dve.tensor_reduce(bmx[:], aux[0:K, 0, 0:P], AX_X, ALU.max).then_inc(bmx_done, 1)
            dve.wait_ge(bmx_done, 1)
            dve.tensor_scalar(bdiag[:], ident[0:K, 0:K], bmx[:, 0:1], None, ALU.mult).then_inc(bdiag_done, 1)
            dve.wait_ge(bmax_mm, 1)
            for i, f in enumerate((1.0, -1.0, 1.0 - SLOPE)):
                dve.tensor_scalar(bmax[:, i, :], aux[:, 1, 0:K], f, None, ALU.mult).then_inc(bmax_done, 1)
            dve.wait_ge(factors_done, 3 * K)
            for k in range(K):
                dve.tensor_copy(v1[:, :, k * VW + D], vall[:, k, :]).then_inc(v1_scaled[0], 1)
            for c in range(NCH):
                hv = v1[:, c * UNR:(c + 1) * UNR, 0:D]
                dve.tensor_tensor(hv, hv, bc(vall[:, 0, c * UNR:(c + 1) * UNR], UNR), ALU.mult)\
                    .then_inc(v1_scaled[0], 1)
            dve.wait_ge(diag_in, 16)
            dve.tensor_scalar(delta[:], adj_diag[:], 0.0, None, ALU.is_le).then_inc(own_done, 1)
            for k in range(K):
                dve.tensor_tensor(coef[:, k, :], wnat[:, k, :], call[:, k, :], ALU.max).then_inc(own_done, 1)
            dve.wait_ge(own_done, 1 + K)
            for k in range(K):
                dve.tensor_tensor(coef[:, k, :], coef[:, k, :], delta[:], ALU.mult).then_inc(own_done, 1)
            dve.wait_ge(own_done, 1 + 2 * K)

            def turn1(b, q, after=None):
                for u in range(UNR):
                    jt = q * UNR + u
                    s = b * NT + jt + S1
                    dve.wait_ge(mask_done, s + 1)
                    dve.wait_ge(pv_done, s + 1)
                    for k in range(K):
                        ins = dve.scalar_tensor_tensor(
                            out=p_sb[:, u % PRING, k, :], in0=v0_flat[:, ds((b % 2) * KB + k * BLK, BLK)],
                            scalar=call[:, k, ds(jt, 1)], in1=maskT[:, u % 2, :], op0=ALU.max, op1=ALU.mult)
                    ins.then_inc(p_made, 1)
                    if u == LAG - 1 and after:
                        after()

            def evacuate1(n):
                dve.wait_ge(pv_done, S1 + n * NT + PRING)
                for k in range(K):
                    for t in range(TPB):
                        row = (n - 1) * TPB + t
                        dve.scalar_tensor_tensor(out=oc[:, k * TPB + t, :], in0=v1_flat[:, ds(row * HW + k * VW, VW)],
                                                 scalar=coef[:, k, ds(row, 1)], in1=acc1(k, t), op0=ALU.mult,
                                                 op1=ALU.add).then_inc(oc1_done, 1)
                dve.wait_ge(oc1_done, n * KT)
                dve.reciprocal(rl[:], oc[:, :, D]).then_inc(rl1_done, 1)

            def stats_att(n):
                dve.wait_ge(att_done, n * K)
                stats(ta, KT, es6, es2, fs6_done, fs2_done, n * KT)

            y = aux[:, :, :].rearrange("p b n -> p (b n)")
            flat = "p t k d -> p (t k d)"

            def elu_min(n):
                dve.wait_ge(y_mm, n)
                dve.tensor_scalar(ymin.rearrange(flat), y, 0.0, None, ALU.min).then_inc(ymin_done, 1)

            def elu_sum(n):
                dve.wait_ge(yexp_done, n)
                dve.scalar_tensor_tensor(out=elu.rearrange(flat), in0=y, scalar=0.0, in1=yexp.rearrange(flat),
                                         op0=ALU.max, op1=ALU.add).then_inc(elu_done, 1)

            dve.wait_ge(w_done, K)
            turn1(0, 0)
            with dve.Fori(1, NQ) as q:
                turn1(0, q)
            with dve.Fori(1, NB) as b:
                dve.wait_ge(w_done, (b + 1) * K)
                turn1(b, 0, lambda: evacuate1(b))
                stats_att(b)
                for i, (lo, hi) in enumerate(SEGS):
                    with dve.Fori(lo, hi) as q:
                        turn1(b, q)
                    if i == 2:
                        elu_min(b)
                    elif i == 3:
                        elu_sum(b)
            evacuate1(NB)
            stats_att(NB)
            elu_min(NB)
            elu_sum(NB)

        @block.tensor
        def _(pe):
            pe.sem_inc(pv_done, PRING)
            pe.wait_ge(ident_set, 2)
            pe.wait_ge(params_in, 8 * 16)
            for k in range(K):
                pe.transpose(aux[:, 0, k * P:(k + 1) * P], w0n[:, k, :], ident[:])
            for k in range(K):
                ins = pe.matmul(aux[:, 0, K * P + 2 * k:K * P + 2 * k + 2], w0n[:, k, :], attn_c[:, k, :],
                                start=True, stop=True)
            ins.then_inc(wprep_mm, 1)
            for k in range(K):
                ins = pe.transpose(aux[:, 1, k * P:(k + 1) * P], w1n[:, k, :], ident[:])
            ins.then_inc(wprep_mm, 1)

            pe.wait_ge(const_set, 4)
            for c in range(NCH):
                pe.wait_ge(h_done, c + 1)
                for t in range(UNR):
                    ins = pe.matmul(acc[:, 2, 0:VW], ones[:], v0[:, c * UNR + t, :], start=(c == 0 and t == 0),
                                    stop=(c == NCH - 1 and t == UNR - 1))
                if c == NCH - 1:
                    ins.then_inc(vsum_mm, 1)
                pe.wait_ge(xhat_done, c + 1)
                for j in range(2):
                    if c:
                        pe.wait_ge(lo_done, 2 * (c - 1) + j + 1)
                    for t in range(TPB):
                        ins = pe.transpose(acc[:, j, t * P:(t + 1) * P], xhat[:, c % 2, j * TPB + t, :], ident[:])
                    ins.then_inc(xT_psum, 1)
            pe.wait_ge(lo_done, 2 * NCH)
            pe.wait_ge(vsum_done, 1)

            def mask_T(bp, q, u):
                slot, j = u // GJ, u % GJ
                if j == 0:
                    pe.wait_ge(adj_in[slot], (bp * NQ + q + 1) * 16)
                pe.wait_ge(p_made, bp * NT + q * UNR + u + 1)
                for t in range(TPB):
                    ins = pe.transpose(maskT[:, u % 2, t * P:(t + 1) * P], adj_sb[:, slot, t, j * P:(j + 1) * P],
                                       ident[:])
                ins.then_inc(mask_done, 1)

            def scores_of(b, q, u):
                keys = ds((q * UNR + u) * P, P)
                rows = ds(b * BLK, BLK)
                if isinstance(b, int) and isinstance(q, int) and b == q == 0 and u < 2:
                    pe.wait_ge(lo_done, 2 * NCH)
                else:
                    pe.wait_ge(exp_done, b * NT + q * UNR + u - 1)
                for i, (kk, rr) in enumerate(((xT_hi, xT_hi), (xT_hi, xT_lo), (xT_lo, xT_hi))):
                    ins = pe.matmul(scores[:, u % 2, :], kk[:, keys], rr[:, rows], start=(i == 0), stop=(i == 2))
                ins.then_inc(scores_done, 1)

            def values0(b, q, u, free=None, last=False):
                s = b * NT + q * UNR + u
                pe.wait_ge(p_made, s + 1 + 2)
                if free:
                    free()
                first = free is not None
                for t in range(TPB):
                    ins = pe.matmul(acc0(t), p_sb[:, u % PRING, 0, t * P:(t + 1) * P],
                                    v0_flat[:, ds((q * UNR + u) * VW, VW)], start=(first and t % 2 == 0), stop=last,
                                    skip_group_check=True)
                ins.then_inc(pv_done, 1)

            def values1(b, q, u, free=None, last=False, scaled=False):
                jt = q * UNR + u
                s = b * NT + jt
                pe.wait_ge(p_made, s + S1 + 1 + 2)
                if free:
                    free()
                if scaled and u == 0:
                    pe.wait_ge(v1_scaled[0], q + 1 + K)
                    pe.wait_ge(v1_scaled[1], q + 1)
                first = free is not None
                for k in range(K):
                    for t in range(TPB):
                        ins = pe.matmul(acc1(k, t), p_sb[:, u % PRING, k, t * P:(t + 1) * P],
                                        v1_flat[:, ds(jt * HW + k * VW, VW)], start=(first and t % 2 == 0),
                                        stop=last, skip_group_check=True)
                ins.then_inc(pv_done, 1)

            def turn(layer, b, q, free=None, flushed=False, scaled=False):
                for u in range(UNR):
                    mask_T(b + layer * NB, q, u)
                    if layer == 0:
                        scores_of(b, q, u)
                    values = values1 if layer else values0
                    kw = dict(scaled=scaled) if layer else {}
                    if u >= LAG:
                        values(b, q, u - LAG, free if u == LAG else None, **kw)
                    elif free is None:
                        values(b, q - 1, u + UNR - LAG, **kw)
                    elif not flushed:
                        values(b - 1, NQ - 1, u + UNR - LAG, last=True)

            def flush(layer):
                for u in range(UNR - LAG, UNR):
                    (values1 if layer else values0)(NB - 1, NQ - 1, u, last=True)

            def ep0_T(n):
                pe.wait_ge(ln_done, n)
                if isinstance(n, int):
                    pe.wait_ge(h_cp, (n - 1) * TPB)
                for t in range(TPB):
                    ins = pe.transpose(aux[:, 0, t * P:(t + 1) * P], tb[:, t, :], ident[:])
                ins.then_inc(lnT_psum, 1)

            def ep0_arow(n):
                pe.wait_ge(lnT_done, n)
                pe.matmul(aux[0:K, 1, :], w_h[:, K * VW:HW], lnT[:, 0, :], start=True, stop=True)\
                    .then_inc(arow_mm, 1)

            def ep0_rows(n, t):
                if t == 1:
                    pe.wait_ge(arow_done, n)
                elif t > 1:
                    pe.wait_ge(h_cp, (n - 1) * TPB + t - 1)
                pe.matmul(aux[:, t % 2, 0:HW], lnT[:, 0, t * P:(t + 1) * P], w_h[:], start=True, stop=True)\
                    .then_inc(h_mm, 1)

            def ep1_T(n):
                pe.wait_ge(ln1_done, n)
                if isinstance(n, int):
                    pe.wait_ge(elu_done, n - 1)
                for k in range(K):
                    for t in range(TPB):
                        ins = pe.transpose(aux[:, k, t * P:(t + 1) * P], tb[:, k * TPB + t, :], ident[:])
                ins.then_inc(attT_psum, 1)

            def ep1_y(n):
                pe.wait_ge(attT_done, n * K)
                for t in range(TPB):
                    for k in range(K):
                        col = (t % 2) * K * D + k * D
                        ins = pe.matmul(aux[:, t // 2, col:col + D], lnT[:, k, t * P:(t + 1) * P], w1T[:, k, :],
                                        start=True, stop=True)
                ins.then_inc(y_mm, 1)

            turn(0, 0, 0, free=lambda: pe.wait_ge(vsum_done, 1), flushed=True)
            with pe.Fori(1, NQ) as q:
                turn(0, 0, q)
            pe.wait_ge(wprep_cp, 3 * K + 1)
            with pe.Fori(1, NB) as b:
                turn(0, b, 0, free=lambda: pe.wait_ge(oc_done, b * TPB))
                for i, (lo, hi) in enumerate(SEGS):
                    with pe.Fori(lo, hi) as q:
                        turn(0, b, q)
                    if i == 1:
                        ep0_T(b)
                    elif i == 2:
                        ep0_arow(b)
                        ep0_rows(b, 0)
                    elif i == 3:
                        for t in range(1, TPB):
                            ep0_rows(b, t)
            flush(0)
            ep0_T(NB)
            ep0_arow(NB)
            for t in range(TPB):
                ep0_rows(NB, t)

            pe.wait_ge(bm_done, K)
            pe.transpose(aux[0:K, 0, 0:P], bm[:], ident[:]).then_inc(bm_T, 1)
            pe.wait_ge(bdiag_done, 1)
            pe.matmul(aux[:, 1, 0:K], ones[0:K, :], bdiag[:], start=True, stop=True).then_inc(bmax_mm, 1)

            turn(1, 0, 0, free=lambda: pe.wait_ge(oc_done, NB * TPB), flushed=True, scaled=True)
            with pe.Fori(1, NQ) as q:
                turn(1, 0, q, scaled=True)
            with pe.Fori(1, NB) as b:
                turn(1, b, 0, free=lambda: pe.wait_ge(oc1_done, b * KT))
                for i, (lo, hi) in enumerate(SEGS):
                    with pe.Fori(lo, hi) as q:
                        turn(1, b, q)
                    if i == 0:
                        ep1_T(b)
                    elif i == 1:
                        ep1_y(b)
            flush(1)
            ep1_T(NB)
            ep1_y(NB)


_INS = ["x", "adj", "L0_gnn_beta", "L1_gnn_ff0_w", "L1_gnn_ff1_w", "L1_gnn_attn_w", "L1_gnn_g1", "L1_gnn_b1",
        "L1_gnn_g2", "L1_gnn_b2"]
_OUTS = [((8192, 128), "float32")]


def kernel(**inputs):
    import numpy as _np
    import concourse.bacc as _bacc
    from concourse import mybir as _mybir
    from concourse.bass_utils import run_bass_kernel_spmd as _run

    nc = _bacc.Bacc("TRN2", target_bir_lowering=False, num_devices=1)
    arrays, args = {}, []
    for name in _INS:
        a = _np.ascontiguousarray(inputs[name])
        arrays[f"in_{name}_dram"] = a
        args.append(nc.dram_tensor(f"in_{name}_dram", a.shape, _mybir.dt.from_np(a.dtype), kind="ExternalInput").ap())
    for i, (shape, dtype) in enumerate(_OUTS):
        dt = _mybir.dt.from_np(_np.dtype(dtype))
        args.append(nc.dram_tensor(f"out_{i}_dram", shape, dt, kind="ExternalOutput").ap())
    adj_prenorm_two_layers(nc, *args)
    r = _run(nc, [arrays], core_ids=[0])
    return r.results[0]["out_0_dram"]
```

```python
import math
from contextlib import ExitStack

import concourse.bass as bass
from concourse import mybir

ALU = mybir.AluOpType
ACT = mybir.ActivationFunctionType
AX_X = mybir.AxisListType.X
F32 = mybir.dt.float32
F16 = mybir.dt.float16
BF16 = mybir.dt.bfloat16
U8 = mybir.dt.uint8
ds = bass.ds

P = 128
TPB = 4
BLK = TPB * P
GJ = 4
SLOTS = 2
UNR = GJ * SLOTS
LAG = (7, 2)
EBUF = 4
PRING = 4
MBUF = 2
NORM_EPS = 1e-7
LN_EPS = 1e-5
SLOPE = 0.01
PSC = 4096.0
XSC = 64.0
SEGS = [(1, 2), (2, 3), (3, 5), (5, 6), (6, 8)]


def adj_prenorm_two_layers(nc, x, adj, beta, ff0_w, ff1_w, attn_w, g1, b1, g2, b2, out):
    N, D = x.shape
    K = ff0_w.shape[0]
    NT = N // P
    NB = N // BLK
    NQ = NT // UNR
    NCH = NQ
    VW = D + 1
    VP = VW + 1
    HW = K * VW + K
    S1 = NB * NT
    KT = K * TPB
    EP0, EP1 = 8, 6
    assert D == P and K == 2 and N % BLK == 0 and SEGS[-1][1] == NQ

    x_t = x.rearrange("(t p) d -> p t d", p=P)
    adj_t = adj.rearrange("(t p) c -> p t c", p=P)
    out_t = out.rearrange("(t p) d -> p t d", p=P)
    mask_d = nc.dram_tensor("mask_scratch", [NB * NQ, P, UNR * BLK], U8, kind="Internal").ap()
    x1_d = nc.dram_tensor("x1_scratch", [N, D], F32, kind="Internal").ap()
    h1_d = nc.dram_tensor("h1_scratch", [N, D], F32, kind="Internal").ap()
    a_d = nc.dram_tensor("src_scratch", [K, N], F32, kind="Internal").ap()
    x1_t = x1_d.rearrange("(t p) d -> p t d", p=P)
    h1_t = h1_d.rearrange("(t p) d -> p t d", p=P)

    with ExitStack() as ctx:
        def sb(name, shape, dt=F32):
            return ctx.enter_context(nc.sbuf_tensor(name, shape, dt))

        def pb(name, shape):
            return ctx.enter_context(nc.psum_tensor(name, shape, F32))

        def sem(name):
            return ctx.enter_context(nc.semaphore(name))

        ident = sb("ident", [P, P])
        ident_b = sb("ident_b", [P, P], BF16)
        ones = sb("ones", [P, P])
        ones_h = sb("ones_h", [P, P], F16)
        neg_half = sb("neg_half", [P, UNR])
        eps_t = sb("eps_t", [P, UNR])
        attn_c = sb("attn_c", [P, K, 2])
        ln_par = sb("ln_par", [P, 4])
        w_h = sb("w_h", [P, HW])
        w1T = sb("w1T", [P, K, D])
        beta_c = sb("beta_c", [P, 1])
        beta_s = sb("beta_s", [P, 1])
        beta_m = sb("beta_m", [P, 1])
        beta_n = sb("beta_n", [P, 1])

        carrier = sb("carrier", [P, 64])

        xT_hi = sb("xT_hi", [P, N], F16)
        xT_lo = sb("xT_lo", [P, N], F16)
        v0_raw = sb("v0_raw", [P, NT * VP])
        v0 = v0_raw[:].bitcast(F16)
        v0_t = v0.rearrange("p (t h d) -> p t h d", h=2, d=VP)
        v1 = sb("v1", [P, NT, HW])
        vsum = sb("vsum", [P, VW])

        adj_sb = sb("adj_sb", [P, SLOTS, TPB, GJ * P])
        m_sb = sb("m_sb", [P, MBUF * UNR * BLK], U8)
        e_sb = sb("e_sb", [P, EBUF, 2 * BLK])
        p_sb = sb("p_sb", [P, PRING, K, BLK])
        p_16 = p_sb[:, :, :, :].rearrange("p r k n -> p (r k n)").bitcast(F16)\
            .rearrange("p (r h n) -> p r h n", r=PRING, h=2)

        v1_flat = v1[:, :, :].rearrange("p t d -> p (t d)")

        def room(flat, start, *dims):
            n = 1
            for d in dims:
                n *= d
            v = flat[:, start:start + n]
            names = "abcd"[:len(dims)]
            return v.rearrange(f"p ({' '.join(names)}) -> p {' '.join(names)}", **dict(zip(names, dims)))

        CW = UNR * D
        xin = room(v1_flat, 0, 2, UNR, D)
        y_c = room(v1_flat, 2 * CW, UNR, D)
        sq_c = room(v1_flat, 3 * CW, UNR, D)
        xhat = room(v1_flat, 4 * CW, 2, UNR, D)
        h_c = room(v1_flat, 6 * CW, 2, UNR, D)
        w0n = room(v1_flat, 8 * CW, K, D)
        w1n = room(v1_flat, 8 * CW + K * D, K, D)
        st6 = sb("st6", [P, UNR, 6])
        st2 = sb("st2", [P, UNR, 2])
        veps = sb("veps", [P, UNR])
        rstd = sb("rstd", [P, UNR])
        n2 = sb("n2", [P, UNR])
        n2e = sb("n2e", [P, UNR])
        rn = sb("rn", [P, UNR])

        oc = sb("oc", [P, KT, VW])
        oc_flat = oc[:, :, :].rearrange("p t d -> p (t d)")
        zrow = sb("zrow", [P, TPB])
        rl = sb("rl", [P, KT])
        xb = sb("xb", [P, TPB, D])
        hb = sb("hb", [P, TPB, D])
        ta0 = sb("ta0", [P, TPB, D])
        tb0 = sb("tb0", [P, TPB, D])
        es6 = sb("es6", [P, KT, 6])
        es2 = sb("es2", [P, KT, 2])
        ever = sb("ever", [P, KT])
        erstd = sb("erstd", [P, KT])
        lnT0 = sb("lnT0", [P, BLK])
        arow = sb("arow", [K, BLK])

        adj_diag = sb("adj_diag", [P, NT])
        bm = sb("bm", [P, K])
        bmx = sb("bmx", [K, 1])
        bdiag = sb("bdiag", [K, K])
        bmax = sb("bmax", [P, 3, K])
        x_flat = xT_hi[:].bitcast(F32)
        KN = K * NT
        vall = room(x_flat, 0, K, NT)
        call = room(x_flat, KN, K, NT)
        wnat = room(x_flat, 2 * KN, K, NT)
        coef = room(x_flat, 3 * KN, K, NT)
        delta = room(x_flat, 4 * KN, NT)

        e_flat = e_sb[:, :, :].rearrange("p r n -> p (r n)")
        ta = room(e_flat, 0, KT, D)
        tb = room(e_flat, KT * D, KT, D)
        lnT = room(e_flat, 2 * KT * D, K, BLK)

        v0_flat = v0_raw[:]
        KB = K * BLK
        w_bc = room(v0_flat, 0, 2 * K, BLK)
        a_bc = room(v0_flat, 2 * KB, K, BLK)
        ymin = room(v0_flat, 3 * KB, TPB, K, D)
        yexp = room(v0_flat, 4 * KB, TPB, K, D)
        elu = room(v0_flat, 5 * KB, TPB, K, D)
        ob = room(v0_flat, 6 * KB, TPB, D)

        maskT = ctx.enter_context(nc.psum_tensor("maskT", [P, 2, 2 * BLK], BF16))
        acc = pb("acc", [P, 4, BLK])
        aux = pb("aux", [P, 2, BLK])

        scores = acc[:, 0:2, :]

        def acc0(t):
            return acc[:, 2 + t // 2, (t % 2) * VW:(t % 2 + 1) * VW]

        def acc1(k, t):
            return acc[:, 2 * k + t // 2, (t % 2) * VW:(t % 2 + 1) * VW]

        ident_set, const_set = sem("ident_set"), sem("const_set")
        params_in, diag_in = sem("params_in"), sem("diag_in")
        wprep_mm, wprep_cp = sem("wprep_mm"), sem("wprep_cp")
        beta_neg, beta_ready = sem("beta_neg"), sem("beta_ready")
        adj_in = [sem(f"adj_in{i}") for i in range(SLOTS)]
        x_in = [sem(f"x_in{i}") for i in range(2)]
        st6_done, st2_done = sem("st6_done"), sem("st2_done")
        veps_done, rstd_done = sem("veps_done"), sem("rstd_done")
        y_done, h_done, sq_done = sem("y_done"), sem("h_done"), sem("sq_done")
        n2_done, n2e_done, rn_done = sem("n2_done"), sem("n2e_done"), sem("rn_done")
        xhat_done, xT_psum = sem("xhat_done"), sem("xT_psum")
        hi_done, lo_done = sem("hi_done"), sem("lo_done")
        vhi_done, vlo_done = sem("vhi_done"), sem("vlo_done")
        vsum_mm, vsum_done = sem("vsum_mm"), sem("vsum_done")
        mask_done = sem("mask_done")
        mcopy_done = sem("mcopy_done")
        mask_out, mask_in = sem("mask_out"), sem("mask_in")
        scores_done = sem("scores_done")
        exp_done = sem("exp_done")
        pw_made, phi_made = sem("pw_made"), sem("phi_made")
        p_made = sem("p_made")
        pv_done = sem("pv_done")
        sums_out = sem("sums_out")
        z_done, oc_done, rl_done = sem("z_done"), sem("oc_done"), sem("rl_done")
        x_blk_in, x1_done, h1_done = sem("x_blk_in"), sem("x1_done"), sem("h1_done")
        ep_chain = sem("ep_chain")
        es6_done, es2_done = sem("es6_done"), sem("es2_done")
        ln_done, lnT_psum, lnT_done = sem("ln_done"), sem("lnT_psum"), sem("lnT_done")
        arow_mm, arow_done = sem("arow_mm"), sem("arow_done")
        h_mm, h_cp = sem("h_mm"), sem("h_cp")
        x1_out, h1_out, a_out = sem("x1_out"), sem("h1_out"), sem("a_out")
        bm_done, bm_T, bmx_done, bdiag_done, bmax_mm, bmax_done = (
            sem("bm_done"), sem("bm_T"), sem("bmx_done"), sem("bdiag_done"), sem("bmax_mm"), sem("bmax_done"))
        factors_done, own_done = sem("factors_done"), sem("own_done")
        v1_scaled = [sem("v1_scaled_h0"), sem("v1_scaled_h1")]
        a_in, w_done = sem("a_in"), sem("w_done")
        oc1_done, rl1_done = sem("oc1_done"), sem("rl1_done")
        x1_back, h1_back = sem("x1_back"), sem("h1_back")
        ep1_chain = sem("ep1_chain")
        att_done = sem("att_done")
        fs6_done, fs2_done = sem("fs6_done"), sem("fs2_done")
        ln1_done, attT_psum, attT_done = sem("ln1_done"), sem("attT_psum"), sem("attT_done")
        y_mm, ymin_done, yexp_done, elu_done = sem("y_mm"), sem("ymin_done"), sem("yexp_done"), sem("elu_done")
        ob_done, out_stored = sem("ob_done"), sem("out_stored")

        block = ctx.enter_context(nc.Block())

        def mask_pair(q, pair):
            return m_sb[:, ds((q % MBUF) * (UNR * BLK) + pair * 2 * BLK, 2 * BLK)]

        def mask_at(q, u):
            return m_sb[:, ds((q % MBUF) * (UNR * BLK) + u * BLK, BLK)]

        carriers = iter(range(64))

        def wait_here(eng, s, value):
            c = next(carriers)
            eng.wait_ge(s, value)
            if eng is nc.vector:
                eng.tensor_copy(carrier[:, c:c + 1], ones[:, 0:1])
            else:
                eng.tensor_tensor(carrier[:, c:c + 1], ones[:, 0:1], ones[:, 0:1], ALU.add)

        def bc(v, n, w=D):
            return v.rearrange("p (t a) -> p t a", a=1).to_broadcast([P, n, w])

        @block.sync
        def _(sp):
            def load_x(c):
                if c >= 2:
                    sp.wait_ge(y_done, c - 1)
                sp.dma_start(xin[:, c % 2], x_t[:, c * UNR:(c + 1) * UNR, :]).then_inc(x_in[c % 2], 16)

            def load_adj(blk, g, slot):
                sp.dma_start(adj_sb[:, slot], adj_t[:, ds(blk * TPB, TPB), ds(g * (GJ * P), GJ * P)])\
                    .then_inc(adj_in[slot], 16)

            load_x(0)
            load_x(1)
            with nc.allow_non_contiguous_dma(reason="small vectors onto partitions"):
                sp.dma_start(beta_c[:], beta.rearrange("(a b) -> a b", a=1).to_broadcast([P, 1]))\
                    .then_inc(params_in, 16)
                sp.dma_start(w0n, ff0_w.rearrange("k o c -> o k c")).then_inc(params_in, 16)
                sp.dma_start(w1n, ff1_w.rearrange("k o c -> o k c")).then_inc(params_in, 16)
                sp.dma_start(attn_c[:], attn_w.rearrange("k (h o) -> o k h", h=2)).then_inc(params_in, 16)
                for i, v in enumerate((g1, b1, g2, b2)):
                    sp.dma_start(ln_par[:, i:i + 1], v.rearrange("(c a) -> c a", a=1)).then_inc(params_in, 16)
            for slot in range(SLOTS):
                load_adj(0, slot, slot)
            for c in range(2, NCH):
                load_x(c)

            def refill(b, q, blk, g0):
                for slot in range(SLOTS):
                    sp.wait_ge(mask_done, b * NT + (q - 1) * UNR + (slot + 1) * GJ)
                    load_adj(blk, g0 + slot, slot)

            with sp.Fori(0, NB - 1) as b:
                with sp.Fori(1, NQ) as q:
                    refill(b, q, b, q * SLOTS)
                refill(b, NQ, b + 1, 0)
            with sp.Fori(1, NQ) as q:
                refill(NB - 1, q, NB - 1, q * SLOTS)

            def load_mask(turn, q):
                sp.dma_start(m_sb[:, ds((q % MBUF) * (UNR * BLK), UNR * BLK)],
                             mask_d[ds(turn, 1)].rearrange("a p n -> (a p) n")).then_inc(mask_in, 16)

            sp.wait_ge(mask_out, NB * NQ * 16)
            sp.wait_ge(p_made, S1 // 2)
            load_mask(0, 0)
            sp.wait_ge(mask_in, 16)
            load_mask(1, 1)
            with sp.Fori(MBUF, NB * NQ) as turn:
                sp.wait_ge(p_made, (turn - 1) * UNR + 1 + S1 // 2)
                load_mask(turn, turn)

        @block.gpsimd
        def _(pool):
            pool.memset(ident[:], 0.0).then_inc(ident_set, 1)
            pool.memset(ones[:], 1.0).then_inc(const_set, 1)
            pool.memset(neg_half[:], -0.5).then_inc(const_set, 1)
            pool.memset(eps_t[:], LN_EPS).then_inc(const_set, 1)
            pool.memset(v0_t[:, :, 0, D:VW], XSC).then_inc(const_set, 1)
            pool.memset(v0_t[:, :, 1, D:VW], 0.0).then_inc(const_set, 1)
            pool.memset(ones_h[:], 1.0).then_inc(const_set, 1)
            pool.wait_ge(ident_set, 1)
            pool.affine_select(out=ident[:], in_=ident[:], compare_op=ALU.not_equal, fill=1.0, base=0,
                               pattern=[[-1, P]], channel_multiplier=1).then_inc(ident_set, 1)
            pool.wait_ge(ident_set, 2)
            pool.tensor_copy(ident_b[:], ident[:]).then_inc(ident_set, 1)
            with nc.allow_non_contiguous_dma(reason="the diagonal of adj"):
                pool.dma_start(adj_diag[:], bass.AP(tensor=adj.tensor, offset=0,
                               ap=[[N + 1, P], [(N + 1) * P, NT]])).then_inc(diag_in, 16)
            pool.wait_ge(const_set, 6)

            def load_a(blk):
                pool.dma_start(a_bc[:, :, :], a_d[:, ds(blk * BLK, BLK)].rearrange("(o k) n -> o k n", o=1)
                               .to_broadcast([P, K, BLK])).then_inc(a_in, 16)

            def link(ins, s, value, carry=False):
                ins.then_inc(s, 1)
                if carry:
                    wait_here(pool, s, value)
                else:
                    pool.wait_ge(s, value)

            for c in range(NCH):
                pool.wait_ge(st2_done, (c + 1) * UNR)
                if c:
                    pool.wait_ge(y_done, c)
                link(pool.tensor_scalar(veps[:], st2[:, :, 1], LN_EPS, None, ALU.add), veps_done, c + 1)
                pool.tensor_tensor(rstd[:], veps[:], neg_half[:], ALU.pow).then_inc(rstd_done, 1)
                pool.wait_ge(n2_done, c + 1)
                link(pool.tensor_scalar(n2e[:], n2[:], NORM_EPS, None, ALU.add), n2e_done, c + 1)
                link(pool.tensor_tensor(rn[:], n2e[:], neg_half[:], ALU.pow), rn_done, c + 1)
                if c >= 2:
                    pool.wait_ge(xT_psum, 2 * (c - 1))
                pool.tensor_tensor(xhat[:, c % 2], h_c[:, c % 2], bc(rn[:], UNR),
                                   ALU.mult).then_inc(xhat_done, 1)

            def epilogue0(n, blk):
                steps = [0]

                def chain(ins, carry=False):
                    steps[0] += 1
                    link(ins, ep_chain, (n - 1) * EP0 + steps[0], carry)

                def inverse_deviations():
                    chain(pool.tensor_tensor(ever[:, 0:TPB], es2[:, 0:TPB, 1], eps_t[:, 0:TPB], ALU.add))
                    chain(pool.tensor_tensor(erstd[:, 0:TPB], ever[:, 0:TPB], neg_half[:, 0:TPB], ALU.pow))

                pool.dma_start(xb[:], x_t[:, ds(blk * TPB, TPB), :]).then_inc(x_blk_in, 16)
                pool.wait_ge(rl_done, n)
                chain(pool.tensor_tensor(ta0[:], oc[:, 0:TPB, 0:D], bc(rl[:, 0:TPB], TPB), ALU.mult))
                pool.wait_ge(x_blk_in, n * 16)
                link(pool.tensor_tensor(xb[:], ta0[:], xb[:], ALU.add), x1_done, n, True)
                pool.dma_start(x1_t[:, ds(blk * TPB, TPB), :], xb[:]).then_inc(x1_out, 16)
                pool.wait_ge(es2_done, n * (2 * TPB) - TPB)
                inverse_deviations()
                chain(pool.tensor_tensor(ta0[:], xb[:], bc(es2[:, 0:TPB, 0], TPB), ALU.subtract))
                chain(pool.tensor_tensor(tb0[:], ta0[:], bc(erstd[:, 0:TPB], TPB), ALU.mult), True)
                link(pool.tensor_scalar(hb[:], tb0[:], 0.0, None, ALU.max), h1_done, n, True)
                pool.dma_start(h1_t[:, ds(blk * TPB, TPB), :], hb[:]).then_inc(h1_out, 16)
                pool.wait_ge(es2_done, n * (2 * TPB))
                inverse_deviations()
                chain(pool.tensor_tensor(ta0[:], hb[:], bc(es2[:, 0:TPB, 0], TPB), ALU.subtract))
                pool.tensor_tensor(tb0[:], ta0[:], bc(erstd[:, 0:TPB], TPB), ALU.mult)\
                    .then_inc(ln_done, 1)
                wait_here(pool, arow_done, n)
                pool.dma_start(a_d[:, ds(blk * BLK, BLK)], arow[:]).then_inc(a_out, 16)
                pool.wait_ge(x1_out, n * 16)
                pool.wait_ge(h1_out, n * 16)
                wait_here(pool, a_out, n * 16)
                assert steps[0] == EP0

            with pool.Fori(0, NB) as blk:
                epilogue0(blk + 1, blk)

            pool.wait_ge(pv_done, S1)
            load_a(0)
            pool.wait_ge(factors_done, 3 * K)
            for c in range(NCH):
                hv = v1[:, c * UNR:(c + 1) * UNR, VW:VW + D]
                pool.tensor_tensor(hv, hv, bc(vall[:, 1, c * UNR:(c + 1) * UNR], UNR), ALU.mult)\
                    .then_inc(v1_scaled[1], 1)

            def epilogue1(n, blk, more):
                steps = [0]

                def chain(ins, carry=False):
                    steps[0] += 1
                    link(ins, ep1_chain, (n - 1) * EP1 + steps[0], carry)

                pool.dma_start(xb[:], x1_t[:, ds(blk * TPB, TPB), :]).then_inc(x1_back, 16)
                pool.dma_start(hb[:], h1_t[:, ds(blk * TPB, TPB), :]).then_inc(h1_back, 16)
                if more:
                    wait_here(pool, w_done, (n + 1) * K)
                    load_a(n + 1)
                pool.wait_ge(rl1_done, n)
                chain(pool.tensor_tensor(ta, oc[:, :, 0:D], bc(rl[:], KT), ALU.mult))
                pool.wait_ge(h1_back, n * 16)
                for k in range(K):
                    pool.tensor_tensor(ta[:, k * TPB:(k + 1) * TPB], ta[:, k * TPB:(k + 1) * TPB], hb[:],
                                       ALU.add).then_inc(att_done, 1)
                pool.wait_ge(fs2_done, n * KT)
                chain(pool.tensor_tensor(ever[:], es2[:, :, 1], eps_t[:, 0:KT], ALU.add))
                chain(pool.tensor_tensor(erstd[:], ever[:], neg_half[:, 0:KT], ALU.pow))
                chain(pool.tensor_tensor(ta, ta, bc(es2[:, :, 0], KT), ALU.subtract))
                pool.tensor_tensor(tb, ta, bc(erstd[:], KT), ALU.mult).then_inc(ln1_done, 1)
                pool.wait_ge(elu_done, n)
                chain(pool.tensor_tensor(ob[:], elu[:, :, 0, :], elu[:, :, 1, :], ALU.add), True)
                chain(pool.tensor_scalar(ob[:], ob[:], 1.0 / K, -1.0, ALU.mult, ALU.add))
                pool.wait_ge(x1_back, n * 16)
                link(pool.tensor_tensor(ob[:], ob[:], xb[:], ALU.add), ob_done, n, True)
                pool.dma_start(out_t[:, ds(blk * TPB, TPB), :], ob[:]).then_inc(out_stored, 16)
                wait_here(pool, out_stored, n * 16)
                assert steps[0] == EP1

            pool.wait_ge(w_done, K)
            load_a(1)
            with pool.Fori(0, NB - 2) as blk:
                epilogue1(blk + 1, blk, True)
            epilogue1(NB - 1, NB - 2, False)
            epilogue1(NB, NB - 1, False)

        @block.scalar
        def _(act):
            act.wait_ge(wprep_mm, 1)
            for k in range(K):
                act.copy(w_h[:, k * VW:k * VW + D], aux[:, 0, k * P:(k + 1) * P]).then_inc(wprep_cp, 1)
                src, dst = K * P + 2 * k, K * P + 2 * k + 1
                act.copy(w_h[:, k * VW + D:(k + 1) * VW], aux[:, 0, dst:dst + 1]).then_inc(wprep_cp, 1)
                act.copy(w_h[:, K * VW + k:K * VW + k + 1], aux[:, 0, src:src + 1]).then_inc(wprep_cp, 1)
            act.wait_ge(wprep_mm, 2)
            act.copy(w1T[:].rearrange("p k d -> p (k d)"), aux[:, 1, 0:K * D]).then_inc(wprep_cp, 1)

            for c in range(NCH):
                act.wait_ge(h_done, c + 1)
                if c:
                    act.wait_ge(n2_done, c)
                act.activation(sq_c, h_c[:, c % 2], ACT.Square).then_inc(sq_done, 1)
                act.activation(v0_t[:, c * UNR:(c + 1) * UNR, 0, 0:D], h_c[:, c % 2], ACT.Copy, scale=XSC)\
                    .then_inc(vhi_done, 1)
                for j in range(2):
                    act.wait_ge(xT_psum, 2 * c + j + 1)
                    col = (2 * c + j) * BLK
                    act.activation(xT_hi[:, col:col + BLK], acc[:, j, :], ACT.Copy, scale=XSC).then_inc(hi_done, 1)
            act.wait_ge(beta_ready, 2)

            def is_zero(b, q):
                return isinstance(b, int) and isinstance(q, int) and b == q == 0

            def store_mask(turn, q):
                act.dma_start(mask_d[ds(turn, 1)].rearrange("a p n -> (a p) n"),
                              m_sb[:, ds((q % MBUF) * (UNR * BLK), UNR * BLK)]).then_inc(mask_out, 16)

            def sums(n, layer):
                act.wait_ge(pv_done, n * NT + layer * S1)
                for i in range(K * (layer + 1)):
                    bank = 2 * (1 - layer) + i
                    act.copy(oc_flat[:, i * 2 * VW:(i + 1) * 2 * VW], acc[:, bank, 0:2 * VW]).then_inc(sums_out, 1)

            def turn0(b, q, first=False, after=None):
                for u in range(UNR):
                    s = b * NT + q * UNR + u
                    if u == 0 and not first and not (is_zero(b, q - 1)):
                        act.wait_ge(mask_out, (b * NQ + q - 1) * 16)
                        act.wait_ge(pw_made, b * (NT // 2) + (q - 1) * (UNR // 2))
                    if u == 2 and not is_zero(b, q):
                        act.wait_ge(mcopy_done, b * (NT // 2) + q * (UNR // 2))
                        store_mask(b * NQ + q - 1, q + NQ - 1)
                    pair = b * (NT // 2) + q * (UNR // 2) + u // 2
                    if u % 2:
                        act.wait_ge(mask_done, s + 1)
                        act.copy(mask_pair(q, u // 2), maskT[:, u // 2 % 2, :]).then_inc(mcopy_done, 1)
                    elif not first:
                        act.wait_ge(p_made, pair - EBUF + 1)
                    act.wait_ge(scores_done, s + 1)
                    act.activation(e_sb[:, u // 2 % EBUF, (u % 2) * BLK:(u % 2 + 1) * BLK], scores[:, u % 2, :], ACT.Exp,
                                   bias=beta_n[:, 0:1], scale=beta_s[:, 0:1]).then_inc(exp_done, 1)
                    if u == LAG[0] - 1 and after:
                        after()

            def normalised(dst, psum, gain):
                return act.activation(dst, psum, ACT.Identity, bias=ln_par[:, gain + 1:gain + 2],
                                      scale=ln_par[:, gain:gain + 1])

            def ep0_norm(n):
                act.wait_ge(lnT_psum, n)
                normalised(lnT0[:], aux[:, 0, :], 0).then_inc(lnT_done, 1)

            def ep0_arow(n):
                act.wait_ge(arow_mm, n)
                act.copy(arow[:], aux[0:K, 1, :]).then_inc(arow_done, 1)

            def ep0_rows(n, t):
                act.wait_ge(h_mm, (n - 1) * TPB + t + 1)
                act.copy(v1_flat[:, ds(((n - 1) * TPB + t) * HW, HW)], aux[:, t % 2, 0:HW]).then_inc(h_cp, 1)

            turn0(0, 0, first=True)
            turn0(0, 1)
            with act.Fori(2, NQ) as q:
                turn0(0, q)
            with act.Fori(1, NB) as b:
                turn0(b, 0, after=lambda: sums(b, 0))
                for i, (lo, hi) in enumerate(SEGS):
                    with act.Fori(lo, hi) as q:
                        turn0(b, q)
                    if i == 2:
                        ep0_norm(b)
                    elif i == 3:
                        ep0_arow(b)
                        ep0_rows(b, 0)
                    elif i == 4:
                        for t in range(1, TPB):
                            ep0_rows(b, t)
            sums(NB, 0)
            act.wait_ge(mcopy_done, S1 // 2)
            act.wait_ge(mask_out, (NB * NQ - 1) * 16)
            store_mask(NB * NQ - 1, NQ - 1)
            ep0_norm(NB)
            ep0_arow(NB)
            for t in range(TPB):
                ep0_rows(NB, t)

            act.wait_ge(bmax_done, 3)
            for k in range(K):
                act.activation(vall[:, k, :], v1[:, :, k * VW + D], ACT.Exp, bias=bmax[:, 1, k:k + 1], scale=1.0)\
                    .then_inc(factors_done, 1)
                act.activation(call[:, k, :], v1[:, :, k * VW + D], ACT.Exp, bias=bmax[:, 2, k:k + 1],
                               scale=-(1.0 - SLOPE)).then_inc(factors_done, 1)
                act.activation(wnat[:, k, :], v1[:, :, K * VW + k], ACT.Exp, bias=bmax[:, 2, k:k + 1],
                               scale=1.0 - SLOPE).then_inc(factors_done, 1)

            def w_block(b):
                act.wait_ge(a_in, (b + 1) * 16)
                for k in range(K):
                    act.activation(v0_flat[:, ds((b % 2) * KB + k * BLK, BLK)], a_bc[:, k, :], ACT.Exp,
                                   bias=bmax[:, 2, k:k + 1], scale=1.0 - SLOPE).then_inc(w_done, 1)

            def ep1(n):
                act.wait_ge(attT_psum, n)
                for k in range(K):
                    normalised(lnT[:, k, :], aux[:, k, :], 2).then_inc(attT_done, 1)
                act.wait_ge(ymin_done, n)
                act.activation(yexp, ymin, ACT.Exp).then_inc(yexp_done, 1)

            w_block(0)
            w_block(1)
            with act.Fori(1, NB - 1) as n:
                sums(n, 1)
                act.wait_ge(p_made, n * NT + S1 // 2)
                w_block(n + 1)
                ep1(n)
            for n in (NB - 1, NB):
                sums(n, 1)
                ep1(n)

        @block.vector
        def _(dve):
            dve.wait_ge(const_set, 6)
            dve.wait_ge(params_in, 8 * 16)
            dve.tensor_scalar(beta_m[:], beta_c[:], 0.0, None, ALU.max).then_inc(beta_neg, 1)
            dve.tensor_scalar(beta_s[:], beta_c[:], 1.0 / (XSC * XSC), None, ALU.mult).then_inc(beta_ready, 1)
            dve.wait_ge(beta_neg, 1)
            dve.tensor_scalar(beta_n[:], beta_m[:], -1.0, math.log(PSC), ALU.mult, ALU.add).then_inc(beta_ready, 1)

            def stats(src, n_tiles, six, two, s6, s2, value6):
                for t in range(n_tiles):
                    dve.bn_stats(six[:, t, :], src[:, t, :]).then_inc(s6, 1)
                wait_here(dve, s6, value6)
                for t in range(n_tiles):
                    dve.bn_aggr(two[:, t, :], six[:, t, :]).then_inc(s2, 1)

            def low_halves(c):
                dve.wait_ge(vhi_done, c + 1)
                vt = v0_t[:, c * UNR:(c + 1) * UNR]
                dve.scalar_tensor_tensor(out=vt[:, :, 1, 0:D], in0=h_c[:, c % 2], scalar=XSC, in1=vt[:, :, 0, 0:D],
                                         op0=ALU.mult, op1=ALU.subtract).then_inc(vlo_done, 1)
                for j in range(2):
                    dve.wait_ge(hi_done, 2 * c + j + 1)
                    col = (2 * c + j) * BLK
                    dve.scalar_tensor_tensor(out=xT_lo[:, col:col + BLK], in0=acc[:, j, :], scalar=XSC,
                                             in1=xT_hi[:, col:col + BLK], op0=ALU.mult, op1=ALU.subtract)\
                        .then_inc(lo_done, 1)

            for c in range(NCH):
                dve.wait_ge(x_in[c % 2], (c // 2 + 1) * 16)
                stats(xin[:, c % 2], UNR, st6, st2, st6_done, st2_done, (c + 1) * UNR)
                dve.wait_ge(rstd_done, c + 1)
                for t in range(UNR):
                    ins = dve.tensor_scalar(y_c[:, t, :], xin[:, c % 2, t, :], st2[:, t, 0:1], rstd[:, t:t + 1],
                                            ALU.subtract, ALU.mult)
                ins.then_inc(y_done, 1)
                dve.wait_ge(y_done, c + 1)
                if c >= 2:
                    dve.wait_ge(xhat_done, c - 1)
                dve.tensor_scalar(h_c[:, c % 2], y_c, 0.0, None, ALU.max).then_inc(h_done, 1)
                dve.wait_ge(sq_done, c + 1)
                dve.tensor_reduce(n2[:], sq_c, AX_X, ALU.add).then_inc(n2_done, 1)
                if c:
                    low_halves(c - 1)
            low_halves(NCH - 1)
            dve.wait_ge(vsum_mm, 1)
            dve.tensor_copy(vsum[:], acc[:, 2, 0:VW]).then_inc(vsum_done, 1)

            def low_weights(pair, r):
                dve.wait_ge(phi_made, pair + 1)
                dve.tensor_tensor(p_16[:, r % PRING, 1, :], e_sb[:, r % EBUF, :], p_16[:, r % PRING, 0, :],
                                  ALU.subtract).then_inc(p_made, 1)

            def turn0(b, q, first=False):
                for r in range(UNR // 2):
                    pair = b * (NT // 2) + q * (UNR // 2) + r
                    e = e_sb[:, r % EBUF, :]
                    dve.wait_ge(exp_done, 2 * pair + 2)
                    dve.wait_ge(mcopy_done, pair + 1)
                    dve.tensor_tensor(e, e, mask_pair(q, r), ALU.mult).then_inc(pw_made, 1)
                    if not (first and r == 0):
                        low_weights(pair - 1, r - 1)
                    if not first:
                        dve.wait_ge(pv_done, 2 * (pair - PRING) + 2)
                    dve.wait_ge(pw_made, pair + 1)
                    dve.tensor_copy(p_16[:, r % PRING, 0, :], e).then_inc(phi_made, 1)

            def no_keys0(n):
                dve.wait_ge(sums_out, 2 * n)
                dve.tensor_scalar(zrow[:], oc[:, 0:TPB, D], 0.0, None, ALU.is_equal).then_inc(z_done, 1)
                dve.wait_ge(z_done, n)
                for t in range(TPB):
                    dve.scalar_tensor_tensor(out=oc[:, t, :], in0=vsum[:], scalar=zrow[:, t:t + 1], in1=oc[:, t, :],
                                             op0=ALU.mult, op1=ALU.add).then_inc(oc_done, 1)
                dve.wait_ge(oc_done, n * TPB)
                dve.reciprocal(rl[:, 0:TPB], oc[:, 0:TPB, D]).then_inc(rl_done, 1)

            def stats_x1(n):
                dve.wait_ge(x1_done, n)
                stats(xb, TPB, es6, es2, es6_done, es2_done, n * (2 * TPB) - TPB)

            def stats_h1(n):
                dve.wait_ge(h1_done, n)
                stats(hb, TPB, es6, es2, es6_done, es2_done, n * (2 * TPB))

            turn0(0, 0, first=True)
            with dve.Fori(1, NQ) as q:
                turn0(0, q)
            with dve.Fori(1, NB) as b:
                turn0(b, 0)
                no_keys0(b)
                for i, (lo, hi) in enumerate(SEGS):
                    with dve.Fori(lo, hi) as q:
                        turn0(b, q)
                    if i == 0:
                        stats_x1(b)
                    elif i == 1:
                        stats_h1(b)
            low_weights(S1 // 2 - 1, UNR // 2 - 1)
            no_keys0(NB)
            stats_x1(NB)
            stats_h1(NB)

            dve.wait_ge(h_cp, NB * TPB)
            for k in range(K):
                dve.tensor_reduce(bm[:, k:k + 1], v1[:, :, k * VW + D], AX_X, ALU.max).then_inc(bm_done, 1)
            dve.wait_ge(bm_T, 1)
            dve.tensor_reduce(bmx[:], aux[0:K, 0, 0:P], AX_X, ALU.max).then_inc(bmx_done, 1)
            dve.wait_ge(bmx_done, 1)
            dve.tensor_scalar(bdiag[:], ident[0:K, 0:K], bmx[:, 0:1], None, ALU.mult).then_inc(bdiag_done, 1)
            dve.wait_ge(bmax_mm, 1)
            for i, f in enumerate((1.0, -1.0, 1.0 - SLOPE)):
                dve.tensor_scalar(bmax[:, i, :], aux[:, 1, 0:K], f, None, ALU.mult).then_inc(bmax_done, 1)
            dve.wait_ge(factors_done, 3 * K)
            for k in range(K):
                dve.tensor_copy(v1[:, :, k * VW + D], vall[:, k, :]).then_inc(v1_scaled[0], 1)
            for c in range(NCH):
                hv = v1[:, c * UNR:(c + 1) * UNR, 0:D]
                dve.tensor_tensor(hv, hv, bc(vall[:, 0, c * UNR:(c + 1) * UNR], UNR), ALU.mult)\
                    .then_inc(v1_scaled[0], 1)
            dve.wait_ge(diag_in, 16)
            dve.tensor_scalar(delta, adj_diag[:], 0.0, None, ALU.is_le).then_inc(own_done, 1)
            for k in range(K):
                dve.tensor_tensor(coef[:, k, :], wnat[:, k, :], call[:, k, :], ALU.max).then_inc(own_done, 1)
            dve.wait_ge(own_done, 1 + K)
            for k in range(K):
                dve.tensor_tensor(coef[:, k, :], coef[:, k, :], delta, ALU.mult).then_inc(own_done, 1)
            dve.wait_ge(own_done, 1 + 2 * K)

            def turn1(b, q):
                for u in range(UNR):
                    jt = q * UNR + u
                    s = b * NT + jt + S1
                    if u == 0:
                        dve.wait_ge(mask_in, (b * NQ + q + 1) * 16)
                    dve.wait_ge(pv_done, s - PRING + 1)
                    for k in range(K):
                        ins = dve.scalar_tensor_tensor(
                            out=p_sb[:, u % PRING, k, :], in0=v0_flat[:, ds((b % 2) * KB + k * BLK, BLK)],
                            scalar=call[:, k, ds(jt, 1)], in1=mask_at(q, u), op0=ALU.max, op1=ALU.mult)
                    ins.then_inc(p_made, 1)

            def own_keys1(n):
                dve.wait_ge(sums_out, 4 * n + 2 * NB)
                for k in range(K):
                    for t in range(TPB):
                        row = (n - 1) * TPB + t
                        dve.scalar_tensor_tensor(out=oc[:, k * TPB + t, :], in0=v1_flat[:, ds(row * HW + k * VW, VW)],
                                                 scalar=coef[:, k, ds(row, 1)], in1=oc[:, k * TPB + t, :], op0=ALU.mult,
                                                 op1=ALU.add).then_inc(oc1_done, 1)
                dve.wait_ge(oc1_done, n * KT)
                dve.reciprocal(rl[:], oc[:, :, D]).then_inc(rl1_done, 1)

            def stats_att(n):
                dve.wait_ge(att_done, n * K)
                stats(ta, KT, es6, es2, fs6_done, fs2_done, n * KT)

            y = aux[:, :, :].rearrange("p b n -> p (b n)")
            flat = "p t k d -> p (t k d)"

            def elu_min(n):
                dve.wait_ge(y_mm, n)
                dve.tensor_scalar(ymin.rearrange(flat), y, 0.0, None, ALU.min).then_inc(ymin_done, 1)

            def elu_sum(n):
                dve.wait_ge(yexp_done, n)
                dve.scalar_tensor_tensor(out=elu.rearrange(flat), in0=y, scalar=0.0, in1=yexp.rearrange(flat),
                                         op0=ALU.max, op1=ALU.add).then_inc(elu_done, 1)

            dve.wait_ge(w_done, K)
            turn1(0, 0)
            with dve.Fori(1, NQ) as q:
                turn1(0, q)
            with dve.Fori(1, NB) as b:
                dve.wait_ge(w_done, (b + 1) * K)
                turn1(b, 0)
                own_keys1(b)
                for i, (lo, hi) in enumerate(SEGS):
                    with dve.Fori(lo, hi) as q:
                        turn1(b, q)
                    if i == 0:
                        stats_att(b)
                    elif i == 3:
                        elu_min(b)
                    elif i == 4:
                        elu_sum(b)
            own_keys1(NB)
            stats_att(NB)
            elu_min(NB)
            elu_sum(NB)

        @block.tensor
        def _(pe):
            pe.wait_ge(ident_set, 3)
            pe.wait_ge(params_in, 8 * 16)
            for k in range(K):
                pe.transpose(aux[:, 0, k * P:(k + 1) * P], w0n[:, k, :], ident[:])
            for k in range(K):
                ins = pe.matmul(aux[:, 0, K * P + 2 * k:K * P + 2 * k + 2], w0n[:, k, :], attn_c[:, k, :],
                                start=True, stop=True)
            ins.then_inc(wprep_mm, 1)
            for k in range(K):
                ins = pe.transpose(aux[:, 1, k * P:(k + 1) * P], w1n[:, k, :], ident[:])
            ins.then_inc(wprep_mm, 1)

            pe.wait_ge(const_set, 6)
            for c in range(NCH):
                pe.wait_ge(xhat_done, c + 1)
                for j in range(2):
                    if c:
                        pe.wait_ge(lo_done, 2 * (c - 1) + j + 1)
                    for t in range(TPB):
                        ins = pe.transpose(acc[:, j, t * P:(t + 1) * P], xhat[:, c % 2, j * TPB + t, :], ident[:])
                    ins.then_inc(xT_psum, 1)
            pe.wait_ge(vlo_done, NCH)
            for t in range(NT):
                for h in range(2):
                    ins = pe.matmul(acc[:, 2, 0:VW], ones_h[:], v0_t[:, t, h, 0:VW], start=(t == 0 and h == 0),
                                    stop=(t == NT - 1 and h == 1))
            ins.then_inc(vsum_mm, 1)
            pe.wait_ge(lo_done, 2 * NCH)

            def is_first(b, q):
                return isinstance(b, int) and isinstance(q, int) and b == q == 0

            def mask_T(b, q, u):
                slot, j = u // GJ, u % GJ
                if j == 0:
                    pe.wait_ge(adj_in[slot], (b * NQ + q + 1) * 16)
                if u % 2 == 0 and not (is_first(b, q) and u < 4):
                    pe.wait_ge(mcopy_done, b * (NT // 2) + q * (UNR // 2) + u // 2 - 1)
                for t in range(TPB):
                    upper = adj_sb[:, slot, t, j * P:(j + 1) * P].bitcast(BF16)[:, 1::2]
                    ins = pe.transpose(maskT[:, u // 2 % 2, (u % 2) * BLK + t * P:(u % 2) * BLK + (t + 1) * P], upper,
                                       ident_b[:])
                ins.then_inc(mask_done, 1)

            def scores_of(b, q, u):
                keys = ds((q * UNR + u) * P, P)
                rows = ds(b * BLK, BLK)
                if is_first(b, q) and u < 2:
                    pe.wait_ge(lo_done, 2 * NCH)
                else:
                    pe.wait_ge(exp_done, b * NT + q * UNR + u - 1)
                for i, (kk, rr) in enumerate(((xT_hi, xT_hi), (xT_hi, xT_lo), (xT_lo, xT_hi))):
                    ins = pe.matmul(scores[:, u % 2, :], kk[:, keys], rr[:, rows], start=(i == 0), stop=(i == 2))
                ins.then_inc(scores_done, 1)

            def values0(b, q, u, free=None, last=False):
                pe.wait_ge(p_made, b * (NT // 2) + q * (UNR // 2) + u // 2 + 1)
                first = free is not None
                weights = p_16[:, u // 2 % PRING, :, (u % 2) * BLK:(u % 2 + 1) * BLK]
                for t in range(TPB):
                    if first and t % 2 == 0:
                        free(t // 2)
                    for i, (wh, vh) in enumerate(((0, 0), (0, 1), (1, 0))):
                        ins = pe.matmul(acc0(t), weights[:, wh, t * P:(t + 1) * P],
                                        v0[:, ds((q * UNR + u) * (2 * VP) + vh * VP, VW)],
                                        start=(first and t % 2 == 0 and i == 0), stop=(last and i == 2),
                                        skip_group_check=True)
                ins.then_inc(pv_done, 1)

            def values1(b, q, u, free=None, last=False, scaled=False):
                jt = q * UNR + u
                s = b * NT + jt
                pe.wait_ge(p_made, s + S1 // 2 + 1)
                if scaled and u == 0:
                    pe.wait_ge(v1_scaled[0], q + 1 + K)
                    pe.wait_ge(v1_scaled[1], q + 1)
                first = free is not None
                for k in range(K):
                    for t in range(TPB):
                        if first and t % 2 == 0:
                            free(2 * k + t // 2)
                        ins = pe.matmul(acc1(k, t), p_sb[:, u % PRING, k, t * P:(t + 1) * P],
                                        v1_flat[:, ds(jt * HW + k * VW, VW)], start=(first and t % 2 == 0),
                                        stop=last, skip_group_check=True)
                ins.then_inc(pv_done, 1)

            def turn(layer, b, q, free=None, flushed=False, scaled=False):
                lag = LAG[layer]
                for u in range(UNR):
                    if layer == 0:
                        mask_T(b, q, u)
                        scores_of(b, q, u)
                    values = values1 if layer else values0
                    kw = dict(scaled=scaled) if layer else {}
                    if u >= lag:
                        values(b, q, u - lag, free if u == lag else None, **kw)
                    elif free is None:
                        values(b, q - 1, u + UNR - lag, **kw)
                    elif not flushed:
                        values(b - 1, NQ - 1, u + UNR - lag, last=True)

            def flush(layer):
                for u in range(UNR - LAG[layer], UNR):
                    (values1 if layer else values0)(NB - 1, NQ - 1, u, last=True)

            def ep0_T(n):
                pe.wait_ge(ln_done, n)
                if isinstance(n, int):
                    pe.wait_ge(h_cp, (n - 1) * TPB)
                for t in range(TPB):
                    ins = pe.transpose(aux[:, 0, t * P:(t + 1) * P], tb0[:, t, :], ident[:])
                ins.then_inc(lnT_psum, 1)

            def ep0_arow(n):
                pe.wait_ge(lnT_done, n)
                pe.matmul(aux[0:K, 1, :], w_h[:, K * VW:HW], lnT0[:], start=True, stop=True)\
                    .then_inc(arow_mm, 1)

            def ep0_rows(n, t):
                if t == 1:
                    pe.wait_ge(arow_done, n)
                elif t > 1:
                    pe.wait_ge(h_cp, (n - 1) * TPB + t - 1)
                pe.matmul(aux[:, t % 2, 0:HW], lnT0[:, t * P:(t + 1) * P], w_h[:], start=True, stop=True)\
                    .then_inc(h_mm, 1)

            def ep1_T(n):
                pe.wait_ge(ln1_done, n)
                if isinstance(n, int):
                    pe.wait_ge(elu_done, n - 1)
                for k in range(K):
                    for t in range(TPB):
                        ins = pe.transpose(aux[:, k, t * P:(t + 1) * P], tb[:, k * TPB + t, :], ident[:])
                ins.then_inc(attT_psum, 1)

            def ep1_y(n):
                pe.wait_ge(attT_done, n * K)
                for t in range(TPB):
                    for k in range(K):
                        col = (t % 2) * K * D + k * D
                        ins = pe.matmul(aux[:, t // 2, col:col + D], lnT[:, k, t * P:(t + 1) * P], w1T[:, k, :],
                                        start=True, stop=True)
                ins.then_inc(y_mm, 1)

            turn(0, 0, 0, free=lambda i: pe.wait_ge(vsum_done, 1), flushed=True)
            with pe.Fori(1, NQ) as q:
                turn(0, 0, q)
            pe.wait_ge(wprep_cp, 3 * K + 1)
            with pe.Fori(1, NB) as b:
                turn(0, b, 0, free=lambda i: pe.wait_ge(sums_out, 2 * b + (i - 1)))
                for i, (lo, hi) in enumerate(SEGS):
                    with pe.Fori(lo, hi) as q:
                        turn(0, b, q)
                    if i == 2:
                        ep0_T(b)
                    elif i == 3:
                        ep0_arow(b)
                        ep0_rows(b, 0)
                    elif i == 4:
                        for t in range(1, TPB):
                            ep0_rows(b, t)
            flush(0)
            ep0_T(NB)
            ep0_arow(NB)
            for t in range(TPB):
                ep0_rows(NB, t)

            pe.wait_ge(bm_done, K)
            pe.transpose(aux[0:K, 0, 0:P], bm[:], ident[:]).then_inc(bm_T, 1)
            pe.wait_ge(bdiag_done, 1)
            pe.matmul(aux[:, 1, 0:K], ones[0:K, :], bdiag[:], start=True, stop=True).then_inc(bmax_mm, 1)

            turn(1, 0, 0, free=lambda i: pe.wait_ge(sums_out, 2 * NB), flushed=True, scaled=True)
            with pe.Fori(1, NQ) as q:
                turn(1, 0, q, scaled=True)
            with pe.Fori(1, NB) as b:
                turn(1, b, 0, free=lambda i: pe.wait_ge(sums_out, 2 * NB + 4 * b + (i - 3)))
                for i, (lo, hi) in enumerate(SEGS):
                    with pe.Fori(lo, hi) as q:
                        turn(1, b, q)
                    if i == 1:
                        ep1_T(b)
                    elif i == 2:
                        ep1_y(b)
            flush(1)
            ep1_T(NB)
            ep1_y(NB)


_INS = ["x", "adj", "L0_gnn_beta", "L1_gnn_ff0_w", "L1_gnn_ff1_w", "L1_gnn_attn_w", "L1_gnn_g1", "L1_gnn_b1",
        "L1_gnn_g2", "L1_gnn_b2"]
_OUTS = [((8192, 128), "float32")]


def kernel(**inputs):
    import numpy as _np
    import concourse.bacc as _bacc
    from concourse import mybir as _mybir
    from concourse.bass_utils import run_bass_kernel_spmd as _run

    nc = _bacc.Bacc("TRN2", target_bir_lowering=False, num_devices=1)
    arrays, args = {}, []
    for name in _INS:
        a = _np.ascontiguousarray(inputs[name])
        arrays[f"in_{name}_dram"] = a
        args.append(nc.dram_tensor(f"in_{name}_dram", a.shape, _mybir.dt.from_np(a.dtype), kind="ExternalInput").ap())
    for i, (shape, dtype) in enumerate(_OUTS):
        dt = _mybir.dt.from_np(_np.dtype(dtype))
        args.append(nc.dram_tensor(f"out_{i}_dram", shape, dt, kind="ExternalOutput").ap())
    adj_prenorm_two_layers(nc, *args)
    r = _run(nc, [arrays], core_ids=[0])
    return r.results[0]["out_0_dram"]
```

```python
import math
from contextlib import ExitStack

import concourse.bass as bass
from concourse import mybir

ALU = mybir.AluOpType
ACT = mybir.ActivationFunctionType
AX_X = mybir.AxisListType.X
F32 = mybir.dt.float32
F16 = mybir.dt.float16
BF16 = mybir.dt.bfloat16
U8 = mybir.dt.uint8
ds = bass.ds

P = 128
TPB = 4
BLK = TPB * P
GJ = 4
SLOTS = 2
UNR = GJ * SLOTS
LAG = (7, 2)
EBUF = 4
PRING = 4
MBUF = 2
NORM_EPS = 1e-7
LN_EPS = 1e-5
SLOPE = 0.01
PSC = 4096.0
XSC = 64.0
SEGS = [(1, 2), (2, 3), (3, 5), (5, 6), (6, 7), (7, 8)]
ROWS_AT = {3: (0, 1), 4: (2, 3)}


def adj_prenorm_two_layers(nc, x, adj, beta, ff0_w, ff1_w, attn_w, g1, b1, g2, b2, out):
    N, D = x.shape
    K = ff0_w.shape[0]
    NT = N // P
    NB = N // BLK
    NQ = NT // UNR
    NCH = NQ
    VW = D + 1
    VP = VW + 1
    HW = K * VW + K
    S1 = NB * NT
    KT = K * TPB
    EP0, EP1 = 8, 4
    assert PRING == EBUF == UNR // 2 and D == P and K == 2 and N % BLK == 0 and SEGS[-1][1] == NQ

    x_t = x.rearrange("(t p) d -> p t d", p=P)
    adj_t = adj.rearrange("(t p) c -> p t c", p=P)
    out_t = out.rearrange("(t p) d -> p t d", p=P)
    mask_d = nc.dram_tensor("mask_scratch", [NB * NQ, P, UNR * BLK], U8, kind="Internal").ap()
    x1_d = nc.dram_tensor("x1_scratch", [N, D], F32, kind="Internal").ap()
    h1_d = nc.dram_tensor("h1_scratch", [N, D], F32, kind="Internal").ap()
    a_d = nc.dram_tensor("src_scratch", [N, K], F32, kind="Internal").ap()
    x1_t = x1_d.rearrange("(t p) d -> p t d", p=P)
    a_t = a_d.rearrange("(t p) k -> p t k", p=P)
    h1_t = h1_d.rearrange("(t p) d -> p t d", p=P)

    with ExitStack() as ctx:
        def sb(name, shape, dt=F32):
            return ctx.enter_context(nc.sbuf_tensor(name, shape, dt))

        def pb(name, shape):
            return ctx.enter_context(nc.psum_tensor(name, shape, F32))

        def sem(name):
            return ctx.enter_context(nc.semaphore(name))

        ident = sb("ident", [P, P])
        ident_b = sb("ident_b", [P, P], BF16)
        ones = sb("ones", [P, P])
        ones_h = sb("ones_h", [P, P], F16)
        neg_half = sb("neg_half", [P, UNR])
        eps_t = sb("eps_t", [P, UNR])
        attn_c = sb("attn_c", [P, K, 2])
        ln_par = sb("ln_par", [P, 4])
        w_h = sb("w_h", [P, HW])
        w1T = sb("w1T", [P, K, D])
        beta_c = sb("beta_c", [P, 1])
        beta_s = sb("beta_s", [P, 1])
        beta_m = sb("beta_m", [P, 1])
        beta_n = sb("beta_n", [P, 1])

        carrier = sb("carrier", [P, 64])

        xT_hi = sb("xT_hi", [P, N], F16)
        xT_lo = sb("xT_lo", [P, N], F16)
        v0_raw = sb("v0_raw", [P, NT * VP])
        v0 = v0_raw[:].bitcast(F16)
        v0_t = v0.rearrange("p (t h d) -> p t h d", h=2, d=VP)
        v1 = sb("v1", [P, NT, HW])
        vsum = sb("vsum", [P, VW])

        adj_sb = sb("adj_sb", [P, SLOTS, TPB, GJ * P])
        m_sb = sb("m_sb", [P, MBUF * UNR * BLK], U8)
        e_sb = sb("e_sb", [P, EBUF, 2 * BLK])
        p_sb = sb("p_sb", [P, PRING, K, BLK])
        p_16 = p_sb[:, :, :, :].rearrange("p r k n -> p (r k n)").bitcast(F16)\
            .rearrange("p (r h n) -> p r h n", r=PRING, h=2)

        v1_flat = v1[:, :, :].rearrange("p t d -> p (t d)")

        def room(flat, start, *dims):
            n = 1
            for d in dims:
                n *= d
            v = flat[:, start:start + n]
            names = "abcd"[:len(dims)]
            return v.rearrange(f"p ({' '.join(names)}) -> p {' '.join(names)}", **dict(zip(names, dims)))

        CW = UNR * D
        xin = room(v1_flat, 0, 2, UNR, D)
        sq_c = room(v1_flat, 3 * CW, UNR, D)
        xhat = room(v1_flat, 4 * CW, 2, UNR, D)
        h_c = room(v1_flat, 6 * CW, 2, UNR, D)
        w0n = room(v1_flat, 8 * CW, K, D)
        w1n = room(v1_flat, 8 * CW + K * D, K, D)
        st6 = sb("st6", [P, 2, UNR, 6])
        st2 = sb("st2", [P, 2, UNR, 2])
        veps = sb("veps", [P, UNR])
        rstd = sb("rstd", [P, 2, UNR])
        shift = sb("shift", [P, 2, UNR])
        n2 = sb("n2", [P, 2, UNR])
        n2e = sb("n2e", [P, UNR])
        rn = sb("rn", [P, UNR])

        oc = sb("oc", [P, KT, VW])
        oc_flat = oc[:, :, :].rearrange("p t d -> p (t d)")
        zrow = sb("zrow", [P, TPB])
        rl = sb("rl", [P, KT])
        xb = sb("xb", [P, TPB, D])
        hb = sb("hb", [P, TPB, D])
        ta0 = sb("ta0", [P, TPB, D])
        tb0 = sb("tb0", [P, TPB, D])
        es6 = sb("es6", [P, KT, 6])
        es2 = sb("es2", [P, KT, 2])
        ever = sb("ever", [P, KT])
        erstd = sb("erstd", [P, KT])
        lnT0 = sb("lnT0", [P, BLK])

        adj_diag = sb("adj_diag", [P, NT])
        bm = sb("bm", [P, K])
        bmx = sb("bmx", [K, 1])
        bdiag = sb("bdiag", [K, K])
        bmax = sb("bmax", [P, 3, K])
        x_flat = xT_hi[:].bitcast(F32)
        KN = K * NT
        vall = room(x_flat, 0, K, NT)
        call = room(x_flat, KN, K, NT)
        wnat = room(x_flat, 2 * KN, K, NT)
        coef = room(x_flat, 3 * KN, K, NT)
        delta = room(x_flat, 4 * KN, NT)

        e_flat = e_sb[:, :, :].rearrange("p r n -> p (r n)")
        ta = room(e_flat, 0, KT, D)
        tb = room(e_flat, KT * D, KT, D)
        lnT = room(e_flat, 2 * KT * D, K, BLK)

        v0_flat = v0_raw[:]
        KB = K * BLK
        a_bc = room(v0_flat, 2 * KB, BLK, K)
        ymin = room(v0_flat, 3 * KB, TPB, K, D)
        yexp = room(v0_flat, 4 * KB, TPB, K, D)
        elu = room(v0_flat, 5 * KB, TPB, K, D)
        ob = room(v0_flat, 6 * KB, TPB, D)
        esum = room(v0_flat, 6 * KB + TPB * D, TPB, D)

        maskT = ctx.enter_context(nc.psum_tensor("maskT", [P, 2, 2 * BLK], BF16))
        acc = pb("acc", [P, 4, BLK])
        aux = pb("aux", [P, 2, BLK])

        scores = acc[:, 0:2, :]

        def acc0(t):
            return acc[:, 2 + t // 2, (t % 2) * VW:(t % 2 + 1) * VW]

        def acc1(k, t):
            return acc[:, 2 * k + t // 2, (t % 2) * VW:(t % 2 + 1) * VW]

        ident_set, const_set = sem("ident_set"), sem("const_set")
        params_in, diag_in = sem("params_in"), sem("diag_in")
        wprep_mm, wprep_cp = sem("wprep_mm"), sem("wprep_cp")
        beta_neg, beta_ready = sem("beta_neg"), sem("beta_ready")
        adj_in = [sem(f"adj_in{i}") for i in range(SLOTS)]
        x_in = [sem(f"x_in{i}") for i in range(2)]
        st6_done, st2_done = sem("st6_done"), sem("st2_done")
        veps_done, rstd_done, mr_done, shift_done = (
            sem("veps_done"), sem("rstd_done"), sem("mr_done"), sem("shift_done"))
        h_done, sq_done = sem("h_done"), sem("sq_done")
        n2_done, n2e_done, rn_done = sem("n2_done"), sem("n2e_done"), sem("rn_done")
        xhat_done, xT_psum = sem("xhat_done"), sem("xT_psum")
        hi_done, lo_done = sem("hi_done"), sem("lo_done")
        vhi_done, vlo_done = sem("vhi_done"), sem("vlo_done")
        vsum_mm, vsum_done = sem("vsum_mm"), sem("vsum_done")
        mask_done = sem("mask_done")
        mcopy_done = sem("mcopy_done")
        mask_out, mask_in = sem("mask_out"), sem("mask_in")
        scores_done = sem("scores_done")
        exp_done = sem("exp_done")
        pw_made, phi_made = sem("pw_made"), sem("phi_made")
        p_made = sem("p_made")
        pv_done = sem("pv_done")
        sums_out = sem("sums_out")
        z_done, oc_done, rl_done = sem("z_done"), sem("oc_done"), sem("rl_done")
        x_blk_in, x1_done, h1_done = sem("x_blk_in"), sem("x1_done"), sem("h1_done")
        ep_chain = sem("ep_chain")
        es6_done, es2_done = sem("es6_done"), sem("es2_done")
        ln_done, lnT_psum, lnT_done = sem("ln_done"), sem("lnT_psum"), sem("lnT_done")
        h_mm, h_cp = sem("h_mm"), sem("h_cp")
        x1_out, h1_out, a_out = sem("x1_out"), sem("h1_out"), sem("a_out")
        bm_done, bm_T, bmx_done, bdiag_done, bmax_mm, bmax_done = (
            sem("bm_done"), sem("bm_T"), sem("bmx_done"), sem("bdiag_done"), sem("bmax_mm"), sem("bmax_done"))
        factors_done, own_done = sem("factors_done"), sem("own_done")
        v1_scaled = [sem("v1_scaled_h0"), sem("v1_scaled_h1")]
        a_in, w_done = sem("a_in"), sem("w_done")
        oc1_done, rl1_done = sem("oc1_done"), sem("rl1_done")
        x1_back, h1_back = sem("x1_back"), sem("h1_back")
        ep1_chain = sem("ep1_chain")
        att_done = sem("att_done")
        fs6_done, fs2_done = sem("fs6_done"), sem("fs2_done")
        ln1_done, attT_psum, attT_done = sem("ln1_done"), sem("attT_psum"), sem("attT_done")
        y_mm, ymin_done, yexp_done, elu_done = sem("y_mm"), sem("ymin_done"), sem("yexp_done"), sem("elu_done")
        last_var, last_rstd, last_norm = sem("last_var"), sem("last_rstd"), sem("last_norm")
        xm_done, esum_done = sem("xm_done"), sem("esum_done")
        ob_done, out_stored = sem("ob_done"), sem("out_stored")

        block = ctx.enter_context(nc.Block())

        def mask_pair(q, pair):
            return m_sb[:, ds((q % MBUF) * (UNR * BLK) + pair * 2 * BLK, 2 * BLK)]

        def mask_at(q, u):
            return m_sb[:, ds((q % MBUF) * (UNR * BLK) + u * BLK, BLK)]

        carriers = iter(range(64))

        def wait_here(eng, s, value):
            c = next(carriers)
            eng.wait_ge(s, value)
            if eng is nc.vector:
                eng.tensor_copy(carrier[:, c:c + 1], ones[:, 0:1])
            elif eng is nc.scalar:
                eng.copy(carrier[:, c:c + 1], ones[:, 0:1])
            else:
                eng.tensor_tensor(carrier[:, c:c + 1], ones[:, 0:1], ones[:, 0:1], ALU.add)

        def bc(v, n, w=D):
            return v.rearrange("p (t a) -> p t a", a=1).to_broadcast([P, n, w])

        @block.sync
        def _(sp):
            def load_x(c):
                if c >= 2:
                    sp.wait_ge(h_done, c - 1)
                sp.dma_start(xin[:, c % 2], x_t[:, c * UNR:(c + 1) * UNR, :]).then_inc(x_in[c % 2], 16)

            def load_adj(blk, g, slot):
                sp.dma_start(adj_sb[:, slot], adj_t[:, ds(blk * TPB, TPB), ds(g * (GJ * P), GJ * P)])\
                    .then_inc(adj_in[slot], 16)

            load_x(0)
            load_x(1)
            with nc.allow_non_contiguous_dma(reason="small vectors onto partitions"):
                sp.dma_start(beta_c[:], beta.rearrange("(a b) -> a b", a=1).to_broadcast([P, 1]))\
                    .then_inc(params_in, 16)
                sp.dma_start(w0n, ff0_w.rearrange("k o c -> o k c")).then_inc(params_in, 16)
                sp.dma_start(w1n, ff1_w.rearrange("k o c -> o k c")).then_inc(params_in, 16)
                sp.dma_start(attn_c[:], attn_w.rearrange("k (h o) -> o k h", h=2)).then_inc(params_in, 16)
                for i, v in enumerate((g1, b1, g2, b2)):
                    sp.dma_start(ln_par[:, i:i + 1], v.rearrange("(c a) -> c a", a=1)).then_inc(params_in, 16)
            for slot in range(SLOTS):
                load_adj(0, slot, slot)
            for c in range(2, NCH):
                load_x(c)

            def refill(b, q, blk, g0):
                for slot in range(SLOTS):
                    sp.wait_ge(mask_done, b * NT + (q - 1) * UNR + (slot + 1) * GJ)
                    load_adj(blk, g0 + slot, slot)

            with sp.Fori(0, NB - 1) as b:
                with sp.Fori(1, NQ) as q:
                    refill(b, q, b, q * SLOTS)
                refill(b, NQ, b + 1, 0)
            with sp.Fori(1, NQ) as q:
                refill(NB - 1, q, NB - 1, q * SLOTS)

            def load_mask(turn, q):
                sp.dma_start(m_sb[:, ds((q % MBUF) * (UNR * BLK), UNR * BLK)],
                             mask_d[ds(turn, 1)].rearrange("a p n -> (a p) n")).then_inc(mask_in, 16)

            sp.wait_ge(mask_out, NB * NQ * 16)
            sp.wait_ge(p_made, S1 // 2)
            load_mask(0, 0)
            sp.wait_ge(mask_in, 16)
            load_mask(1, 1)
            with sp.Fori(MBUF, NB * NQ) as turn:
                sp.wait_ge(p_made, (turn - 1) * UNR + 1 + S1 // 2)
                load_mask(turn, turn)

        @block.gpsimd
        def _(pool):
            pool.memset(ident[:], 0.0).then_inc(ident_set, 1)
            pool.memset(ones[:], 1.0).then_inc(const_set, 1)
            pool.memset(neg_half[:], -0.5).then_inc(const_set, 1)
            pool.memset(eps_t[:], LN_EPS).then_inc(const_set, 1)
            pool.memset(v0_t[:, :, 0, D:VW], XSC).then_inc(const_set, 1)
            pool.memset(v0_t[:, :, 1, D:VW], 0.0).then_inc(const_set, 1)
            pool.memset(ones_h[:], 1.0).then_inc(const_set, 1)
            pool.wait_ge(ident_set, 1)
            pool.affine_select(out=ident[:], in_=ident[:], compare_op=ALU.not_equal, fill=1.0, base=0,
                               pattern=[[-1, P]], channel_multiplier=1).then_inc(ident_set, 1)
            pool.wait_ge(ident_set, 2)
            pool.tensor_copy(ident_b[:], ident[:]).then_inc(ident_set, 1)
            with nc.allow_non_contiguous_dma(reason="the diagonal of adj"):
                pool.dma_start(adj_diag[:], bass.AP(tensor=adj.tensor, offset=0,
                               ap=[[N + 1, P], [(N + 1) * P, NT]])).then_inc(diag_in, 16)
            pool.wait_ge(const_set, 6)

            def link(ins, s, value, carry=False):
                ins.then_inc(s, 1)
                if carry:
                    wait_here(pool, s, value)
                else:
                    pool.wait_ge(s, value)

            def deviations(c):
                i = c % 2
                pool.wait_ge(st2_done, (c + 1) * UNR)
                if c >= 2:
                    pool.wait_ge(h_done, c - 1)
                link(pool.tensor_scalar(veps[:], st2[:, i, :, 1], LN_EPS, None, ALU.add), veps_done, c + 1)
                link(pool.tensor_tensor(rstd[:, i], veps[:], neg_half[:], ALU.pow), rstd_done, c + 1)
                link(pool.tensor_tensor(shift[:, i], st2[:, i, :, 0], rstd[:, i], ALU.mult), mr_done, c + 1)
                pool.tensor_scalar(shift[:, i], shift[:, i], -1.0, None, ALU.mult).then_inc(shift_done, 1)

            def unit_rows(c):
                pool.wait_ge(n2_done, c + 1)
                link(pool.tensor_scalar(n2e[:], n2[:, c % 2], NORM_EPS, None, ALU.add), n2e_done, c + 1)
                link(pool.tensor_tensor(rn[:], n2e[:], neg_half[:], ALU.pow), rn_done, c + 1)
                if c >= 2:
                    pool.wait_ge(xT_psum, 2 * (c - 1))
                pool.tensor_tensor(xhat[:, c % 2], h_c[:, c % 2], bc(rn[:], UNR),
                                   ALU.mult).then_inc(xhat_done, 1)

            deviations(0)
            for c in range(NCH):
                if c + 1 < NCH:
                    deviations(c + 1)
                unit_rows(c)

            def epilogue0(n, blk):
                steps = [0]

                def chain(ins, carry=False):
                    steps[0] += 1
                    link(ins, ep_chain, (n - 1) * EP0 + steps[0], carry)

                def inverse_deviations():
                    chain(pool.tensor_tensor(ever[:, 0:TPB], es2[:, 0:TPB, 1], eps_t[:, 0:TPB], ALU.add))
                    chain(pool.tensor_tensor(erstd[:, 0:TPB], ever[:, 0:TPB], neg_half[:, 0:TPB], ALU.pow))

                pool.dma_start(xb[:], x_t[:, ds(blk * TPB, TPB), :]).then_inc(x_blk_in, 16)
                pool.wait_ge(rl_done, n)
                chain(pool.tensor_tensor(ta0[:], oc[:, 0:TPB, 0:D], bc(rl[:, 0:TPB], TPB), ALU.mult))
                pool.wait_ge(x_blk_in, n * 16)
                link(pool.tensor_tensor(xb[:], ta0[:], xb[:], ALU.add), x1_done, n, True)
                pool.dma_start(x1_t[:, ds(blk * TPB, TPB), :], xb[:]).then_inc(x1_out, 16)
                pool.wait_ge(es2_done, n * (2 * TPB) - TPB)
                inverse_deviations()
                chain(pool.tensor_tensor(ta0[:], xb[:], bc(es2[:, 0:TPB, 0], TPB), ALU.subtract))
                chain(pool.tensor_tensor(tb0[:], ta0[:], bc(erstd[:, 0:TPB], TPB), ALU.mult), True)
                link(pool.tensor_scalar(hb[:], tb0[:], 0.0, None, ALU.max), h1_done, n, True)
                pool.dma_start(h1_t[:, ds(blk * TPB, TPB), :], hb[:]).then_inc(h1_out, 16)
                pool.wait_ge(es2_done, n * (2 * TPB))
                inverse_deviations()
                chain(pool.tensor_tensor(ta0[:], hb[:], bc(es2[:, 0:TPB, 0], TPB), ALU.subtract))
                pool.tensor_tensor(tb0[:], ta0[:], bc(erstd[:, 0:TPB], TPB), ALU.mult)\
                    .then_inc(ln_done, 1)
                wait_here(pool, h_cp, n * TPB)
                with nc.allow_non_contiguous_dma(reason="two source scores a row"):
                    pool.dma_start(a_t[:, ds(blk * TPB, TPB), :], v1[:, ds(blk * TPB, TPB), K * VW:HW])\
                        .then_inc(a_out, 16)
                assert steps[0] == EP0

            def last0(n, blk):
                def inverse_deviations(step):
                    pool.wait_ge(es2_done, n * (2 * TPB) - (2 - step) * TPB)
                    link(pool.tensor_tensor(ever[:, 0:TPB], es2[:, 0:TPB, 1], eps_t[:, 0:TPB], ALU.add), last_var,
                         step)
                    pool.tensor_tensor(erstd[:, 0:TPB], ever[:, 0:TPB], neg_half[:, 0:TPB], ALU.pow)\
                        .then_inc(last_rstd, 1)

                pool.dma_start(xb[:], x_t[:, blk * TPB:(blk + 1) * TPB, :]).then_inc(x_blk_in, 16)
                inverse_deviations(1)
                pool.wait_ge(x1_done, n)
                pool.dma_start(x1_t[:, blk * TPB:(blk + 1) * TPB, :], xb[:]).then_inc(x1_out, 16)
                inverse_deviations(2)
                pool.wait_ge(h1_done, n)
                pool.dma_start(h1_t[:, blk * TPB:(blk + 1) * TPB, :], hb[:]).then_inc(h1_out, 16)
                pool.wait_ge(h_cp, n * TPB)
                with nc.allow_non_contiguous_dma(reason="two source scores a row"):
                    pool.dma_start(a_t[:, blk * TPB:(blk + 1) * TPB, :],
                                   v1[:, blk * TPB:(blk + 1) * TPB, K * VW:HW]).then_inc(a_out, 16)

            def stores_landed(n):
                pool.wait_ge(x1_out, n * 16)
                pool.wait_ge(h1_out, n * 16)
                wait_here(pool, a_out, n * 16)

            with pool.Fori(0, NB - 1) as blk:
                epilogue0(blk + 1, blk)
                stores_landed(blk + 1)
            last0(NB, NB - 1)

            pool.wait_ge(factors_done, 3 * K)
            for c in range(NCH):
                hv = v1[:, c * UNR:(c + 1) * UNR, VW:VW + D]
                pool.tensor_tensor(hv, hv, bc(vall[:, 1, c * UNR:(c + 1) * UNR], UNR), ALU.mult)\
                    .then_inc(v1_scaled[1], 1)

            def epilogue1(n, blk):
                steps = [0]

                def chain(ins, carry=False):
                    steps[0] += 1
                    link(ins, ep1_chain, (n - 1) * EP1 + steps[0], carry)

                pool.dma_start(xb[:], x1_t[:, ds(blk * TPB, TPB), :]).then_inc(x1_back, 16)
                pool.dma_start(hb[:], h1_t[:, ds(blk * TPB, TPB), :]).then_inc(h1_back, 16)
                pool.wait_ge(rl1_done, n)
                chain(pool.tensor_tensor(ta, oc[:, :, 0:D], bc(rl[:], KT), ALU.mult))
                pool.wait_ge(h1_back, n * 16)
                for k in range(K):
                    pool.tensor_tensor(ta[:, k * TPB:(k + 1) * TPB], ta[:, k * TPB:(k + 1) * TPB], hb[:],
                                       ALU.add).then_inc(att_done, 1)
                pool.wait_ge(fs2_done, n * KT)
                chain(pool.tensor_tensor(ever[:], es2[:, :, 1], eps_t[:, 0:KT], ALU.add))
                chain(pool.tensor_tensor(erstd[:], ever[:], neg_half[:, 0:KT], ALU.pow))
                chain(pool.tensor_tensor(ta, ta, bc(es2[:, :, 0], KT), ALU.subtract))
                pool.tensor_tensor(tb, ta, bc(erstd[:], KT), ALU.mult).then_inc(ln1_done, 1)
                wait_here(pool, x1_back, n * 16)
                pool.tensor_scalar(xb[:], xb[:], -1.0, None, ALU.add).then_inc(xm_done, 1)
                wait_here(pool, ob_done, n)
                assert steps[0] == EP1

            def last1(n, blk):
                pool.dma_start(hb[:], h1_t[:, blk * TPB:(blk + 1) * TPB, :]).then_inc(h1_back, 16)
                pool.dma_start(xb[:], x1_t[:, blk * TPB:(blk + 1) * TPB, :]).then_inc(x1_back, 16)
                pool.wait_ge(fs2_done, n * KT)
                link(pool.tensor_tensor(ever[:], es2[:, :, 1], eps_t[:, 0:KT], ALU.add), last_var, 3)
                pool.tensor_tensor(erstd[:], ever[:], neg_half[:, 0:KT], ALU.pow).then_inc(last_rstd, 1)
                pool.wait_ge(x1_back, n * 16)
                pool.tensor_scalar(xb[:], xb[:], -1.0, None, ALU.add).then_inc(xm_done, 1)

            stores_landed(NB)
            with pool.Fori(0, NB - 1) as blk:
                epilogue1(blk + 1, blk)
            last1(NB, NB - 1)

        @block.scalar
        def _(act):
            act.wait_ge(wprep_mm, 1)
            for k in range(K):
                act.copy(w_h[:, k * VW:k * VW + D], aux[:, 0, k * P:(k + 1) * P]).then_inc(wprep_cp, 1)
                src, dst = K * P + 2 * k, K * P + 2 * k + 1
                act.copy(w_h[:, k * VW + D:(k + 1) * VW], aux[:, 0, dst:dst + 1]).then_inc(wprep_cp, 1)
                act.copy(w_h[:, K * VW + k:K * VW + k + 1], aux[:, 0, src:src + 1]).then_inc(wprep_cp, 1)
            act.wait_ge(wprep_mm, 2)
            act.copy(w1T[:].rearrange("p k d -> p (k d)"), aux[:, 1, 0:K * D]).then_inc(wprep_cp, 1)

            def high_halves(c):
                for j in range(2):
                    act.wait_ge(xT_psum, 2 * c + j + 1)
                    col = (2 * c + j) * BLK
                    act.activation(xT_hi[:, col:col + BLK], acc[:, 2 * (c % 2) + j, :], ACT.Copy, scale=XSC)\
                        .then_inc(hi_done, 1)

            for c in range(NCH):
                act.wait_ge(shift_done, c + 1)
                act.wait_ge(x_in[c % 2], (c // 2 + 1) * 16)
                if c >= 2:
                    act.wait_ge(xhat_done, c - 1)
                    act.wait_ge(vlo_done, c - 1)
                for t in range(UNR):
                    ins = act.activation(h_c[:, c % 2, t, :], xin[:, c % 2, t, :], ACT.Relu,
                                         bias=shift[:, c % 2, t:t + 1], scale=rstd[:, c % 2, t:t + 1])
                ins.then_inc(h_done, 1)
                act.wait_ge(h_done, c + 1)
                if c:
                    act.wait_ge(n2_done, c)
                act.activation(sq_c, h_c[:, c % 2], ACT.Square).then_inc(sq_done, 1)
                act.activation(v0_t[:, c * UNR:(c + 1) * UNR, 0, 0:D], h_c[:, c % 2], ACT.Copy, scale=XSC)\
                    .then_inc(vhi_done, 1)
                if c:
                    high_halves(c - 1)
            high_halves(NCH - 1)
            act.wait_ge(beta_ready, 2)

            def is_zero(b, q):
                return isinstance(b, int) and isinstance(q, int) and b == q == 0

            def store_mask(turn, q):
                act.dma_start(mask_d[ds(turn, 1)].rearrange("a p n -> (a p) n"),
                              m_sb[:, ds((q % MBUF) * (UNR * BLK), UNR * BLK)]).then_inc(mask_out, 16)

            def load_a(blk):
                act.dma_start(a_bc[:, :, :], a_d[ds(blk * BLK, BLK)].rearrange("(o n) k -> o n k", o=1)
                              .to_broadcast([P, BLK, K])).then_inc(a_in, 16)

            def sums(n, layer):
                act.wait_ge(pv_done, n * NT + layer * S1)
                for i in range(K * (layer + 1)):
                    bank = 2 * (1 - layer) + i
                    act.copy(oc_flat[:, i * 2 * VW:(i + 1) * 2 * VW], acc[:, bank, 0:2 * VW]).then_inc(sums_out, 1)

            def last_high_weights(pair, first):
                act.wait_ge(pw_made, pair + 1)
                if not first:
                    act.wait_ge(pv_done, 2 * (pair - PRING) + 2)
                act.copy(p_16[:, PRING - 1, 0, :], e_sb[:, EBUF - 1, :]).then_inc(phi_made, 1)

            def turn0(b, q, first=False, after=None):
                for u in range(UNR):
                    s = b * NT + q * UNR + u
                    if u == 0 and not first and not (is_zero(b, q - 1)):
                        act.wait_ge(mask_out, (b * NQ + q - 1) * 16)
                        act.wait_ge(pw_made, b * (NT // 2) + (q - 1) * (UNR // 2))
                    if u == 2 and not is_zero(b, q):
                        act.wait_ge(mcopy_done, b * (NT // 2) + q * (UNR // 2))
                        store_mask(b * NQ + q - 1, q + NQ - 1)
                    pair = b * (NT // 2) + q * (UNR // 2) + u // 2
                    if u % 2:
                        act.wait_ge(mask_done, s + 1)
                        act.copy(mask_pair(q, u // 2), maskT[:, u // 2 % 2, :]).then_inc(mcopy_done, 1)
                    elif not first:
                        act.wait_ge(p_made, pair - EBUF + 1)
                    act.wait_ge(scores_done, s + 1)
                    act.activation(e_sb[:, u // 2 % EBUF, (u % 2) * BLK:(u % 2 + 1) * BLK], scores[:, u % 2, :], ACT.Exp,
                                   bias=beta_n[:, 0:1], scale=beta_s[:, 0:1]).then_inc(exp_done, 1)
                    if u == 1 and not is_zero(b, q):
                        last_high_weights(pair - 1, is_zero(b, q - 1))
                    if u == LAG[0] - 1 and after:
                        after()

            def normalised(dst, psum, gain):
                return act.activation(dst, psum, ACT.Identity, bias=ln_par[:, gain + 1:gain + 2],
                                      scale=ln_par[:, gain:gain + 1])

            def ep0_norm(n):
                act.wait_ge(lnT_psum, n)
                normalised(lnT0[:], aux[:, 0, :], 0).then_inc(lnT_done, 1)

            def ep0_rows(n, t):
                act.wait_ge(h_mm, (n - 1) * TPB + t + 1)
                act.copy(v1_flat[:, ds(((n - 1) * TPB + t) * HW, HW)], aux[:, t % 2, 0:HW]).then_inc(h_cp, 1)

            turn0(0, 0, first=True)
            turn0(0, 1)
            with act.Fori(2, NQ) as q:
                turn0(0, q)
            with act.Fori(1, NB) as b:
                turn0(b, 0, after=lambda: sums(b, 0))
                for i, (lo, hi) in enumerate(SEGS):
                    with act.Fori(lo, hi) as q:
                        turn0(b, q)
                    if i == 2:
                        ep0_norm(b)
                    elif i in (3, 4):
                        for t in ROWS_AT[i]:
                            ep0_rows(b, t)
            last_high_weights(S1 // 2 - 1, False)
            sums(NB, 0)
            act.wait_ge(a_out, 16)
            load_a(0)
            act.wait_ge(mcopy_done, S1 // 2)
            act.wait_ge(mask_out, (NB * NQ - 1) * 16)
            store_mask(NB * NQ - 1, NQ - 1)
            ep0_norm(NB)
            for t in range(TPB):
                ep0_rows(NB, t)

            act.wait_ge(bmax_done, 3)
            for k in range(K):
                act.activation(vall[:, k, :], v1[:, :, k * VW + D], ACT.Exp, bias=bmax[:, 1, k:k + 1], scale=1.0)\
                    .then_inc(factors_done, 1)
                act.activation(call[:, k, :], v1[:, :, k * VW + D], ACT.Exp, bias=bmax[:, 2, k:k + 1],
                               scale=-(1.0 - SLOPE)).then_inc(factors_done, 1)
                act.activation(wnat[:, k, :], v1[:, :, K * VW + k], ACT.Exp, bias=bmax[:, 2, k:k + 1],
                               scale=1.0 - SLOPE).then_inc(factors_done, 1)

            def w_block(b):
                if not isinstance(b, int) or b > 0:
                    act.wait_ge(w_done, b * K)
                    load_a(b)
                act.wait_ge(a_in, (b + 1) * 16)
                for k in range(K):
                    act.activation(v0_flat[:, ds((b % 2) * KB + k * BLK, BLK)], a_bc[:, :, k], ACT.Exp,
                                   bias=bmax[:, 2, k:k + 1], scale=1.0 - SLOPE).then_inc(w_done, 1)

            def ep1(n):
                act.wait_ge(attT_psum, n)
                for k in range(K):
                    normalised(lnT[:, k, :], aux[:, k, :], 2).then_inc(attT_done, 1)
                act.wait_ge(ymin_done, n)
                act.activation(yexp, ymin, ACT.Exp).then_inc(yexp_done, 1)
                act.wait_ge(ob_done, n)
                act.dma_start(out_t[:, ds((n - 1) * TPB, TPB), :], ob).then_inc(out_stored, 16)
                wait_here(act, out_stored, n * 16)

            w_block(0)
            w_block(1)
            with act.Fori(1, NB - 1) as n:
                sums(n, 1)
                act.wait_ge(p_made, n * NT + S1 // 2)
                w_block(n + 1)
                ep1(n)
            for n in (NB - 1, NB):
                sums(n, 1)
                ep1(n)

        @block.vector
        def _(dve):
            dve.wait_ge(const_set, 6)
            dve.wait_ge(params_in, 8 * 16)
            dve.tensor_scalar(beta_m[:], beta_c[:], 0.0, None, ALU.max).then_inc(beta_neg, 1)
            dve.tensor_scalar(beta_s[:], beta_c[:], 1.0 / (XSC * XSC), None, ALU.mult).then_inc(beta_ready, 1)
            dve.wait_ge(beta_neg, 1)
            dve.tensor_scalar(beta_n[:], beta_m[:], -1.0, math.log(PSC), ALU.mult, ALU.add).then_inc(beta_ready, 1)

            def stats(src, n_tiles, six, two, s6, s2, value6):
                for t in range(n_tiles):
                    dve.bn_stats(six[:, t, :], src[:, t, :]).then_inc(s6, 1)
                wait_here(dve, s6, value6)
                for t in range(n_tiles):
                    dve.bn_aggr(two[:, t, :], six[:, t, :]).then_inc(s2, 1)

            def low_values(c):
                dve.wait_ge(vhi_done, c + 1)
                vt = v0_t[:, c * UNR:(c + 1) * UNR]
                dve.scalar_tensor_tensor(out=vt[:, :, 1, 0:D], in0=h_c[:, c % 2], scalar=XSC, in1=vt[:, :, 0, 0:D],
                                         op0=ALU.mult, op1=ALU.subtract).then_inc(vlo_done, 1)

            def low_rows(c):
                for j in range(2):
                    dve.wait_ge(hi_done, 2 * c + j + 1)
                    col = (2 * c + j) * BLK
                    dve.scalar_tensor_tensor(out=xT_lo[:, col:col + BLK], in0=acc[:, 2 * (c % 2) + j, :], scalar=XSC,
                                             in1=xT_hi[:, col:col + BLK], op0=ALU.mult, op1=ALU.subtract)\
                        .then_inc(lo_done, 1)

            def stats_x(c):
                dve.wait_ge(x_in[c % 2], (c // 2 + 1) * 16)
                if c >= 2:
                    dve.wait_ge(st2_done, (c - 1) * UNR)
                    dve.wait_ge(shift_done, c - 1)
                stats(xin[:, c % 2], UNR, st6[:, c % 2], st2[:, c % 2], st6_done, st2_done, (c + 1) * UNR)

            stats_x(0)
            for c in range(NCH):
                if c + 1 < NCH:
                    stats_x(c + 1)
                dve.wait_ge(sq_done, c + 1)
                dve.tensor_reduce(n2[:, c % 2], sq_c, AX_X, ALU.add).then_inc(n2_done, 1)
                low_values(c)
                if c:
                    low_rows(c - 1)
            low_rows(NCH - 1)

            def low_weights(pair, r):
                dve.wait_ge(phi_made, pair + 1)
                dve.tensor_tensor(p_16[:, r % PRING, 1, :], e_sb[:, r % EBUF, :], p_16[:, r % PRING, 0, :],
                                  ALU.subtract).then_inc(p_made, 1)

            def turn0(b, q, first=False):
                for r in range(UNR // 2):
                    pair = b * (NT // 2) + q * (UNR // 2) + r
                    e = e_sb[:, r % EBUF, :]
                    dve.wait_ge(exp_done, 2 * pair + 2)
                    dve.wait_ge(mcopy_done, pair + 1)
                    dve.tensor_tensor(e, e, mask_pair(q, r), ALU.mult).then_inc(pw_made, 1)
                    if not (first and r == 0):
                        low_weights(pair - 1, r - 1)
                    if r == UNR // 2 - 1:
                        continue
                    if not first:
                        dve.wait_ge(pv_done, 2 * (pair - PRING) + 2)
                    dve.wait_ge(pw_made, pair + 1)
                    dve.tensor_copy(p_16[:, r % PRING, 0, :], e).then_inc(phi_made, 1)

            def no_keys0(n):
                dve.wait_ge(sums_out, 2 * n)
                dve.tensor_scalar(zrow[:], oc[:, 0:TPB, D], 0.0, None, ALU.is_equal).then_inc(z_done, 1)
                dve.wait_ge(z_done, n)
                for t in range(TPB):
                    dve.scalar_tensor_tensor(out=oc[:, t, :], in0=vsum[:], scalar=zrow[:, t:t + 1], in1=oc[:, t, :],
                                             op0=ALU.mult, op1=ALU.add).then_inc(oc_done, 1)
                dve.wait_ge(oc_done, n * TPB)
                dve.reciprocal(rl[:, 0:TPB], oc[:, 0:TPB, D]).then_inc(rl_done, 1)

            def stats_x1(n):
                dve.wait_ge(x1_done, n)
                stats(xb, TPB, es6, es2, es6_done, es2_done, n * (2 * TPB) - TPB)

            def stats_h1(n):
                dve.wait_ge(h1_done, n)
                stats(hb, TPB, es6, es2, es6_done, es2_done, n * (2 * TPB))

            turn0(0, 0, first=True)
            dve.wait_ge(vsum_mm, 1)
            dve.tensor_copy(vsum[:], aux[:, 0, 0:VW]).then_inc(vsum_done, 1)
            with dve.Fori(1, NQ) as q:
                turn0(0, q)
            dve.wait_ge(vsum_done, 1)
            with dve.Fori(1, NB) as b:
                turn0(b, 0)
                no_keys0(b)
                for i, (lo, hi) in enumerate(SEGS):
                    with dve.Fori(lo, hi) as q:
                        turn0(b, q)
                    if i == 0:
                        stats_x1(b)
                    elif i == 1:
                        stats_h1(b)
            low_weights(S1 // 2 - 1, UNR // 2 - 1)
            no_keys0(NB)

            def add_scaled(dst, n_tiles, base):
                dve.wait_ge(rl1_done if n_tiles == KT else rl_done, NB)
                for t in range(n_tiles):
                    ins = dve.scalar_tensor_tensor(out=dst[:, t, :], in0=oc[:, t, 0:D], scalar=rl[:, t:t + 1],
                                                   in1=base[:, t % TPB, :], op0=ALU.mult, op1=ALU.add)
                return ins

            def normalise(dst, src, n_tiles, step):
                dve.wait_ge(last_rstd, step)
                for t in range(n_tiles):
                    ins = dve.tensor_scalar(dst[:, t, :], src[:, t, :], es2[:, t, 0:1], erstd[:, t:t + 1],
                                            ALU.subtract, ALU.mult)
                return ins

            dve.wait_ge(x_blk_in, NB * 16)
            add_scaled(xb, TPB, xb).then_inc(x1_done, 1)
            stats_x1(NB)
            normalise(tb0, xb, TPB, 1).then_inc(last_norm, 1)
            dve.wait_ge(last_norm, 1)
            dve.tensor_scalar(hb[:], tb0[:], 0.0, None, ALU.max).then_inc(h1_done, 1)
            stats_h1(NB)
            normalise(tb0, hb, TPB, 2).then_inc(ln_done, 1)

            dve.wait_ge(h_cp, NB * TPB)
            for k in range(K):
                dve.tensor_reduce(bm[:, k:k + 1], v1[:, :, k * VW + D], AX_X, ALU.max).then_inc(bm_done, 1)
            dve.wait_ge(bm_T, 1)
            dve.tensor_reduce(bmx[:], aux[0:K, 0, 0:P], AX_X, ALU.max).then_inc(bmx_done, 1)
            dve.wait_ge(bmx_done, 1)
            dve.tensor_scalar(bdiag[:], ident[0:K, 0:K], bmx[:, 0:1], None, ALU.mult).then_inc(bdiag_done, 1)
            dve.wait_ge(bmax_mm, 1)
            for i, f in enumerate((1.0, -1.0, 1.0 - SLOPE)):
                dve.tensor_scalar(bmax[:, i, :], aux[:, 1, 0:K], f, None, ALU.mult).then_inc(bmax_done, 1)
            dve.wait_ge(factors_done, 3 * K)
            for k in range(K):
                dve.tensor_copy(v1[:, :, k * VW + D], vall[:, k, :]).then_inc(v1_scaled[0], 1)

            def scale_values(c):
                hv = v1_flat[:, ds(c * (UNR * HW), UNR * HW)].rearrange("p (t d) -> p t d", d=HW)[:, :, 0:D]
                dve.tensor_tensor(hv, hv, bc(vall[:, 0, ds(c * UNR, UNR)], UNR), ALU.mult).then_inc(v1_scaled[0], 1)

            def own_weights():
                dve.wait_ge(diag_in, 16)
                dve.tensor_scalar(delta, adj_diag[:], 0.0, None, ALU.is_le).then_inc(own_done, 1)
                for k in range(K):
                    dve.tensor_tensor(coef[:, k, :], wnat[:, k, :], call[:, k, :], ALU.max).then_inc(own_done, 1)
                dve.wait_ge(own_done, 1 + K)
                for k in range(K):
                    dve.tensor_tensor(coef[:, k, :], coef[:, k, :], delta, ALU.mult).then_inc(own_done, 1)

            def turn1(b, q):
                for u in range(UNR):
                    jt = q * UNR + u
                    s = b * NT + jt + S1
                    if u == 0:
                        dve.wait_ge(mask_in, (b * NQ + q + 1) * 16)
                    dve.wait_ge(pv_done, s - PRING + 1)
                    for k in range(K):
                        ins = dve.scalar_tensor_tensor(
                            out=p_sb[:, u % PRING, k, :], in0=v0_flat[:, ds((b % 2) * KB + k * BLK, BLK)],
                            scalar=call[:, k, ds(jt, 1)], in1=mask_at(q, u), op0=ALU.max, op1=ALU.mult)
                    ins.then_inc(p_made, 1)

            def own_keys1(n):
                dve.wait_ge(sums_out, 4 * n + 2 * NB)
                for k in range(K):
                    for t in range(TPB):
                        row = (n - 1) * TPB + t
                        dve.scalar_tensor_tensor(out=oc[:, k * TPB + t, :], in0=v1_flat[:, ds(row * HW + k * VW, VW)],
                                                 scalar=coef[:, k, ds(row, 1)], in1=oc[:, k * TPB + t, :], op0=ALU.mult,
                                                 op1=ALU.add).then_inc(oc1_done, 1)
                dve.wait_ge(oc1_done, n * KT)
                dve.reciprocal(rl[:], oc[:, :, D]).then_inc(rl1_done, 1)

            def stats_att(n):
                dve.wait_ge(att_done, n * K)
                stats(ta, KT, es6, es2, fs6_done, fs2_done, n * KT)

            y = aux[:, :, :].rearrange("p b n -> p (b n)")
            flat = "p t k d -> p (t k d)"

            def elu_min(n):
                dve.wait_ge(y_mm, n)
                dve.tensor_scalar(ymin.rearrange(flat), y, 0.0, None, ALU.min).then_inc(ymin_done, 1)

            def elu_sum(n):
                dve.wait_ge(yexp_done, n)
                dve.scalar_tensor_tensor(out=elu.rearrange(flat), in0=y, scalar=0.0, in1=yexp.rearrange(flat),
                                         op0=ALU.max, op1=ALU.add).then_inc(elu_done, 1)
                dve.wait_ge(elu_done, n)
                dve.tensor_tensor(esum, elu[:, :, 0, :], elu[:, :, 1, :], ALU.add).then_inc(esum_done, 1)
                dve.wait_ge(esum_done, n)
                dve.wait_ge(xm_done, n)
                dve.scalar_tensor_tensor(out=ob, in0=esum, scalar=1.0 / K, in1=xb[:], op0=ALU.mult,
                                         op1=ALU.add).then_inc(ob_done, 1)

            dve.wait_ge(w_done, K)
            scale_values(0)
            turn1(0, 0)
            own_weights()
            with dve.Fori(1, NQ) as q:
                scale_values(q)
                turn1(0, q)
            dve.wait_ge(own_done, 1 + 2 * K)
            with dve.Fori(1, NB) as b:
                dve.wait_ge(w_done, (b + 1) * K)
                turn1(b, 0)
                own_keys1(b)
                for i, (lo, hi) in enumerate(SEGS):
                    with dve.Fori(lo, hi) as q:
                        turn1(b, q)
                    if i == 0:
                        stats_att(b)
                    elif i == 3:
                        elu_min(b)
                    elif i == 4:
                        elu_sum(b)
            own_keys1(NB)
            dve.wait_ge(h1_back, NB * 16)
            add_scaled(ta, KT, hb).then_inc(att_done, K)
            stats_att(NB)
            normalise(tb, ta, KT, 3).then_inc(ln1_done, 1)
            elu_min(NB)
            elu_sum(NB)

        @block.tensor
        def _(pe):
            pe.wait_ge(ident_set, 3)
            pe.wait_ge(params_in, 8 * 16)
            for k in range(K):
                pe.transpose(aux[:, 0, k * P:(k + 1) * P], w0n[:, k, :], ident[:])
            for k in range(K):
                ins = pe.matmul(aux[:, 0, K * P + 2 * k:K * P + 2 * k + 2], w0n[:, k, :], attn_c[:, k, :],
                                start=True, stop=True)
            ins.then_inc(wprep_mm, 1)
            for k in range(K):
                ins = pe.transpose(aux[:, 1, k * P:(k + 1) * P], w1n[:, k, :], ident[:])
            ins.then_inc(wprep_mm, 1)

            def sum_values(c):
                pe.wait_ge(vlo_done, c + 1)
                for t in range(c * UNR, (c + 1) * UNR):
                    for h in range(2):
                        ins = pe.matmul(aux[:, 0, 0:VW], ones_h[:], v0_t[:, t, h, 0:VW], start=(t == 0 and h == 0),
                                        stop=(t == NT - 1 and h == 1))
                return ins

            pe.wait_ge(const_set, 6)
            pe.wait_ge(wprep_cp, 3 * K + 1)
            for c in range(NCH):
                pe.wait_ge(xhat_done, c + 1)
                for j in range(2):
                    if c >= 2:
                        pe.wait_ge(lo_done, 2 * (c - 2) + j + 1)
                    for t in range(TPB):
                        ins = pe.transpose(acc[:, 2 * (c % 2) + j, t * P:(t + 1) * P],
                                           xhat[:, c % 2, j * TPB + t, :], ident[:])
                    ins.then_inc(xT_psum, 1)
                ins = sum_values(c)
            ins.then_inc(vsum_mm, 1)
            pe.wait_ge(lo_done, 2 * NCH)

            def is_first(b, q):
                return isinstance(b, int) and isinstance(q, int) and b == q == 0

            def mask_T(b, q, u):
                slot, j = u // GJ, u % GJ
                if j == 0:
                    pe.wait_ge(adj_in[slot], (b * NQ + q + 1) * 16)
                if u % 2 == 0 and not (is_first(b, q) and u < 4):
                    pe.wait_ge(mcopy_done, b * (NT // 2) + q * (UNR // 2) + u // 2 - 1)
                for t in range(TPB):
                    upper = adj_sb[:, slot, t, j * P:(j + 1) * P].bitcast(BF16)[:, 1::2]
                    ins = pe.transpose(maskT[:, u // 2 % 2, (u % 2) * BLK + t * P:(u % 2) * BLK + (t + 1) * P], upper,
                                       ident_b[:])
                ins.then_inc(mask_done, 1)

            def scores_of(b, q, u):
                keys = ds((q * UNR + u) * P, P)
                rows = ds(b * BLK, BLK)
                if is_first(b, q) and u < 2:
                    pe.wait_ge(lo_done, 2 * NCH)
                else:
                    pe.wait_ge(exp_done, b * NT + q * UNR + u - 1)
                for i, (kk, rr) in enumerate(((xT_hi, xT_hi), (xT_hi, xT_lo), (xT_lo, xT_hi))):
                    ins = pe.matmul(scores[:, u % 2, :], kk[:, keys], rr[:, rows], start=(i == 0), stop=(i == 2))
                ins.then_inc(scores_done, 1)

            def values0(b, q, u, free=None, last=False):
                pe.wait_ge(p_made, b * (NT // 2) + q * (UNR // 2) + u // 2 + 1)
                first = free is not None
                weights = p_16[:, u // 2 % PRING, :, (u % 2) * BLK:(u % 2 + 1) * BLK]
                for t in range(TPB):
                    if first and t % 2 == 0:
                        free(t // 2)
                    for i, (wh, vh) in enumerate(((0, 0), (0, 1), (1, 0))):
                        ins = pe.matmul(acc0(t), weights[:, wh, t * P:(t + 1) * P],
                                        v0[:, ds((q * UNR + u) * (2 * VP) + vh * VP, VW)],
                                        start=(first and t % 2 == 0 and i == 0), stop=(last and i == 2),
                                        skip_group_check=True)
                ins.then_inc(pv_done, 1)

            def values1(b, q, u, free=None, last=False, scaled=False):
                jt = q * UNR + u
                s = b * NT + jt
                pe.wait_ge(p_made, s + S1 // 2 + 1)
                if scaled and u == 0:
                    pe.wait_ge(v1_scaled[0], q + 1 + K)
                    pe.wait_ge(v1_scaled[1], q + 1)
                first = free is not None
                for k in range(K):
                    for t in range(TPB):
                        if first and t % 2 == 0:
                            free(2 * k + t // 2)
                        ins = pe.matmul(acc1(k, t), p_sb[:, u % PRING, k, t * P:(t + 1) * P],
                                        v1_flat[:, ds(jt * HW + k * VW, VW)], start=(first and t % 2 == 0),
                                        stop=last, skip_group_check=True)
                ins.then_inc(pv_done, 1)

            def turn(layer, b, q, free=None, flushed=False, scaled=False):
                lag = LAG[layer]
                for u in range(UNR):
                    if layer == 0:
                        mask_T(b, q, u)
                        scores_of(b, q, u)
                    values = values1 if layer else values0
                    kw = dict(scaled=scaled) if layer else {}
                    if u >= lag:
                        values(b, q, u - lag, free if u == lag else None, **kw)
                    elif free is None:
                        values(b, q - 1, u + UNR - lag, **kw)
                    elif not flushed:
                        values(b - 1, NQ - 1, u + UNR - lag, last=True)

            def flush(layer):
                for u in range(UNR - LAG[layer], UNR):
                    (values1 if layer else values0)(NB - 1, NQ - 1, u, last=True)

            def ep0_T(n):
                pe.wait_ge(ln_done, n)
                if isinstance(n, int):
                    pe.wait_ge(h_cp, (n - 1) * TPB)
                for t in range(TPB):
                    ins = pe.transpose(aux[:, 0, t * P:(t + 1) * P], tb0[:, t, :], ident[:])
                ins.then_inc(lnT_psum, 1)

            def ep0_rows(n, t):
                if t == 0:
                    pe.wait_ge(lnT_done, n)
                elif t > 1:
                    pe.wait_ge(h_cp, (n - 1) * TPB + t - 1)
                pe.matmul(aux[:, t % 2, 0:HW], lnT0[:, t * P:(t + 1) * P], w_h[:], start=True, stop=True)\
                    .then_inc(h_mm, 1)

            def ep1_T(n):
                pe.wait_ge(ln1_done, n)
                if isinstance(n, int):
                    pe.wait_ge(elu_done, n - 1)
                for k in range(K):
                    for t in range(TPB):
                        ins = pe.transpose(aux[:, k, t * P:(t + 1) * P], tb[:, k * TPB + t, :], ident[:])
                ins.then_inc(attT_psum, 1)

            def ep1_y(n):
                pe.wait_ge(attT_done, n * K)
                for t in range(TPB):
                    for k in range(K):
                        col = (t % 2) * K * D + k * D
                        ins = pe.matmul(aux[:, t // 2, col:col + D], lnT[:, k, t * P:(t + 1) * P], w1T[:, k, :],
                                        start=True, stop=True)
                ins.then_inc(y_mm, 1)

            turn(0, 0, 0, free=lambda i: pe.wait_ge(lo_done, 2 * NCH), flushed=True)
            with pe.Fori(1, NQ) as q:
                turn(0, 0, q)
            with pe.Fori(1, NB) as b:
                turn(0, b, 0, free=lambda i: pe.wait_ge(sums_out, 2 * b + (i - 1)))
                for i, (lo, hi) in enumerate(SEGS):
                    with pe.Fori(lo, hi) as q:
                        turn(0, b, q)
                    if i == 2:
                        ep0_T(b)
                    elif i in (3, 4):
                        for t in ROWS_AT[i]:
                            ep0_rows(b, t)
            flush(0)
            ep0_T(NB)
            for t in range(TPB):
                ep0_rows(NB, t)

            pe.wait_ge(bm_done, K)
            pe.transpose(aux[0:K, 0, 0:P], bm[:], ident[:]).then_inc(bm_T, 1)
            pe.wait_ge(bdiag_done, 1)
            pe.matmul(aux[:, 1, 0:K], ones[0:K, :], bdiag[:], start=True, stop=True).then_inc(bmax_mm, 1)

            turn(1, 0, 0, free=lambda i: pe.wait_ge(sums_out, 2 * NB), flushed=True, scaled=True)
            with pe.Fori(1, NQ) as q:
                turn(1, 0, q, scaled=True)
            with pe.Fori(1, NB) as b:
                turn(1, b, 0, free=lambda i: pe.wait_ge(sums_out, 2 * NB + 4 * b + (i - 3)))
                for i, (lo, hi) in enumerate(SEGS):
                    with pe.Fori(lo, hi) as q:
                        turn(1, b, q)
                    if i == 1:
                        ep1_T(b)
                    elif i == 2:
                        ep1_y(b)
            flush(1)
            ep1_T(NB)
            ep1_y(NB)


_INS = ["x", "adj", "L0_gnn_beta", "L1_gnn_ff0_w", "L1_gnn_ff1_w", "L1_gnn_attn_w", "L1_gnn_g1", "L1_gnn_b1",
        "L1_gnn_g2", "L1_gnn_b2"]
_OUTS = [((8192, 128), "float32")]


def kernel(**inputs):
    import numpy as _np
    import concourse.bacc as _bacc
    from concourse import mybir as _mybir
    from concourse.bass_utils import run_bass_kernel_spmd as _run

    nc = _bacc.Bacc("TRN2", target_bir_lowering=False, num_devices=1)
    arrays, args = {}, []
    for name in _INS:
        a = _np.ascontiguousarray(inputs[name])
        arrays[f"in_{name}_dram"] = a
        args.append(nc.dram_tensor(f"in_{name}_dram", a.shape, _mybir.dt.from_np(a.dtype), kind="ExternalInput").ap())
    for i, (shape, dtype) in enumerate(_OUTS):
        dt = _mybir.dt.from_np(_np.dtype(dtype))
        args.append(nc.dram_tensor(f"out_{i}_dram", shape, dt, kind="ExternalOutput").ap())
    adj_prenorm_two_layers(nc, *args)
    r = _run(nc, [arrays], core_ids=[0])
    return r.results[0]["out_0_dram"]
```
